# Optimizing a Trainium2 kernel written in Bass

```python
import numpy as np
import jax
import jax.numpy as jnp

def _softmax(x, axis=-1):
    return jax.nn.softmax(x, axis=axis)

def _gelu(x):
    return jax.nn.gelu(x, approximate=True)

def _silu(x):
    return jax.nn.silu(x)

def _sigmoid(x):
    return jax.nn.sigmoid(x)

def _layernorm(x, axis=-1, eps=1e-05):
    m = jnp.mean(x, axis=axis, keepdims=True)
    v = jnp.var(x, axis=axis, keepdims=True)
    return (x - m) / jnp.sqrt(v + eps)

def _scatter_add(tgt, idx, src, axis=0):
    return tgt.at[idx].add(src)

def _segment_sum(src, seg, n):
    return jax.ops.segment_sum(src, seg, n)
kernel_name = 'mk_dlrm_tower_d1_rec_r8_05922e'

def setup_inputs(seed: int=0):
    np.random.seed(seed)
    _w = jnp.asarray

    def _rec_inputs():
        import jax
        import jax.numpy as jnp
        _tk = jax.random.key(seed)
        dense_ctx = jax.random.normal(jax.random.fold_in(_tk, 190), (512, 16), jnp.float32)
        ids = jnp.stack([jax.random.randint(jax.random.fold_in(_tk, 200 + f), (512,), 0, v, jnp.int32) for f, v in enumerate([125000, 125000, 125000, 12500, 12500, 12500, 125000, 12500, 125000, 12500, 1250, 12500, 125000, 1000, 12500, 125000, 12500, 125000, 125000, 125000, 125000, 125000, 125000, 125000, 1250, 1000, 1250, 1000, 1000, 12500, 12500, 1000, 1000, 1000, 1250, 1000, 1000, 1000, 12500])], axis=1)
        tbl_0 = 0.05 * jax.random.normal(jax.random.fold_in(_tk, 500 + 0), (125000, 16), jnp.float32)
        tbl_1 = 0.05 * jax.random.normal(jax.random.fold_in(_tk, 500 + 1), (125000, 16), jnp.float32)
        tbl_2 = 0.05 * jax.random.normal(jax.random.fold_in(_tk, 500 + 2), (125000, 16), jnp.float32)
        tbl_3 = 0.05 * jax.random.normal(jax.random.fold_in(_tk, 500 + 3), (12500, 16), jnp.float32)
        tbl_4 = 0.05 * jax.random.normal(jax.random.fold_in(_tk, 500 + 4), (12500, 16), jnp.float32)
        tbl_5 = 0.05 * jax.random.normal(jax.random.fold_in(_tk, 500 + 5), (12500, 16), jnp.float32)
        tbl_6 = 0.05 * jax.random.normal(jax.random.fold_in(_tk, 500 + 6), (125000, 16), jnp.float32)
        tbl_7 = 0.05 * jax.random.normal(jax.random.fold_in(_tk, 500 + 7), (12500, 16), jnp.float32)
        tbl_8 = 0.05 * jax.random.normal(jax.random.fold_in(_tk, 500 + 8), (125000, 16), jnp.float32)
        tbl_9 = 0.05 * jax.random.normal(jax.random.fold_in(_tk, 500 + 9), (12500, 16), jnp.float32)
        tbl_10 = 0.05 * jax.random.normal(jax.random.fold_in(_tk, 500 + 10), (1250, 16), jnp.float32)
        tbl_11 = 0.05 * jax.random.normal(jax.random.fold_in(_tk, 500 + 11), (12500, 16), jnp.float32)
        tbl_12 = 0.05 * jax.random.normal(jax.random.fold_in(_tk, 500 + 12), (125000, 16), jnp.float32)
        tbl_13 = 0.05 * jax.random.normal(jax.random.fold_in(_tk, 500 + 13), (1000, 16), jnp.float32)
        tbl_14 = 0.05 * jax.random.normal(jax.random.fold_in(_tk, 500 + 14), (12500, 16), jnp.float32)
        tbl_15 = 0.05 * jax.random.normal(jax.random.fold_in(_tk, 500 + 15), (125000, 16), jnp.float32)
        tbl_16 = 0.05 * jax.random.normal(jax.random.fold_in(_tk, 500 + 16), (12500, 16), jnp.float32)
        tbl_17 = 0.05 * jax.random.normal(jax.random.fold_in(_tk, 500 + 17), (125000, 16), jnp.float32)
        tbl_18 = 0.05 * jax.random.normal(jax.random.fold_in(_tk, 500 + 18), (125000, 16), jnp.float32)
        tbl_19 = 0.05 * jax.random.normal(jax.random.fold_in(_tk, 500 + 19), (125000, 16), jnp.float32)
        tbl_20 = 0.05 * jax.random.normal(jax.random.fold_in(_tk, 500 + 20), (125000, 16), jnp.float32)
        tbl_21 = 0.05 * jax.random.normal(jax.random.fold_in(_tk, 500 + 21), (125000, 16), jnp.float32)
        tbl_22 = 0.05 * jax.random.normal(jax.random.fold_in(_tk, 500 + 22), (125000, 16), jnp.float32)
        tbl_23 = 0.05 * jax.random.normal(jax.random.fold_in(_tk, 500 + 23), (125000, 16), jnp.float32)
        tbl_24 = 0.05 * jax.random.normal(jax.random.fold_in(_tk, 500 + 24), (1250, 16), jnp.float32)
        tbl_25 = 0.05 * jax.random.normal(jax.random.fold_in(_tk, 500 + 25), (1000, 16), jnp.float32)
        tbl_26 = 0.05 * jax.random.normal(jax.random.fold_in(_tk, 500 + 26), (1250, 16), jnp.float32)
        tbl_27 = 0.05 * jax.random.normal(jax.random.fold_in(_tk, 500 + 27), (1000, 16), jnp.float32)
        tbl_28 = 0.05 * jax.random.normal(jax.random.fold_in(_tk, 500 + 28), (1000, 16), jnp.float32)
        tbl_29 = 0.05 * jax.random.normal(jax.random.fold_in(_tk, 500 + 29), (12500, 16), jnp.float32)
        tbl_30 = 0.05 * jax.random.normal(jax.random.fold_in(_tk, 500 + 30), (12500, 16), jnp.float32)
        tbl_31 = 0.05 * jax.random.normal(jax.random.fold_in(_tk, 500 + 31), (1000, 16), jnp.float32)
        tbl_32 = 0.05 * jax.random.normal(jax.random.fold_in(_tk, 500 + 32), (1000, 16), jnp.float32)
        tbl_33 = 0.05 * jax.random.normal(jax.random.fold_in(_tk, 500 + 33), (1000, 16), jnp.float32)
        tbl_34 = 0.05 * jax.random.normal(jax.random.fold_in(_tk, 500 + 34), (1250, 16), jnp.float32)
        tbl_35 = 0.05 * jax.random.normal(jax.random.fold_in(_tk, 500 + 35), (1000, 16), jnp.float32)
        tbl_36 = 0.05 * jax.random.normal(jax.random.fold_in(_tk, 500 + 36), (1000, 16), jnp.float32)
        tbl_37 = 0.05 * jax.random.normal(jax.random.fold_in(_tk, 500 + 37), (1000, 16), jnp.float32)
        tbl_38 = 0.05 * jax.random.normal(jax.random.fold_in(_tk, 500 + 38), (12500, 16), jnp.float32)
        _rk = jax.random.fold_in(_tk, 7)
        W_top1 = 0.05 * jax.random.normal(jax.random.fold_in(_tk, 801), (400, 512), jnp.float32)
        W_top2 = 0.0441942 * jax.random.normal(jax.random.fold_in(_tk, 802), (512, 256), jnp.float32)
        W_top3 = 0.0625 * jax.random.normal(jax.random.fold_in(_tk, 803), (256, 1), jnp.float32)
        b_top1 = jnp.zeros((512,), jnp.float32)
        b_top2 = jnp.zeros((256,), jnp.float32)
        return (dense_ctx, ids, tbl_0, tbl_1, tbl_2, tbl_3, tbl_4, tbl_5, tbl_6, tbl_7, tbl_8, tbl_9, tbl_10, tbl_11, tbl_12, tbl_13, tbl_14, tbl_15, tbl_16, tbl_17, tbl_18, tbl_19, tbl_20, tbl_21, tbl_22, tbl_23, tbl_24, tbl_25, tbl_26, tbl_27, tbl_28, tbl_29, tbl_30, tbl_31, tbl_32, tbl_33, tbl_34, tbl_35, tbl_36, tbl_37, tbl_38, W_top1, b_top1, W_top2, b_top2, W_top3)
    dense_ctx, ids, tbl_0, tbl_1, tbl_2, tbl_3, tbl_4, tbl_5, tbl_6, tbl_7, tbl_8, tbl_9, tbl_10, tbl_11, tbl_12, tbl_13, tbl_14, tbl_15, tbl_16, tbl_17, tbl_18, tbl_19, tbl_20, tbl_21, tbl_22, tbl_23, tbl_24, tbl_25, tbl_26, tbl_27, tbl_28, tbl_29, tbl_30, tbl_31, tbl_32, tbl_33, tbl_34, tbl_35, tbl_36, tbl_37, tbl_38, W_top1, b_top1, W_top2, b_top2, W_top3 = _rec_inputs()

    def _L0_rec_setup():
        import jax, jax.numpy as jnp
        import numpy as np
        B, F0, D = (512, 39, 16)
        CIN = [128, 128, 128]

        def _cin_layer(X0, Xi, W, b):
            H = W.shape[0]
            F0_, Fi = (X0.shape[1], Xi.shape[1])
            Wr = W.reshape(H, F0_, Fi)
            return jnp.einsum('hjk,bjd,bkd->bhd', Wr, X0, Xi) + b[None, :, None]
        key = jax.random.key(seed)
        ks = jax.random.split(key, 4)
        x = jax.random.normal(ks[0], (B, F0, D), dtype=jnp.float32)
        fields = [F0] + CIN
        inp = {'embedded_features': x}
        for i in range(len(CIN)):
            cin = F0 * fields[i]
            cout = fields[i + 1]
            kw = jax.random.fold_in(ks[1], i)
            inp[f'W{i}'] = jax.random.normal(kw, (cout, cin), dtype=jnp.float32) / np.sqrt(cin)
            inp[f'b{i}'] = jnp.zeros((cout,), dtype=jnp.float32)
        return inp
    _L0_rec_all = _L0_rec_setup()
    _L0_rec_in = {k: v for k, v in _L0_rec_all.items() if k in ('W0', 'b0', 'W1', 'b1', 'W2', 'b2')}
    del _L0_rec_all
    return {'dense_ctx': dense_ctx, 'ids': ids, 'tbl_0': tbl_0, 'tbl_1': tbl_1, 'tbl_2': tbl_2, 'tbl_3': tbl_3, 'tbl_4': tbl_4, 'tbl_5': tbl_5, 'tbl_6': tbl_6, 'tbl_7': tbl_7, 'tbl_8': tbl_8, 'tbl_9': tbl_9, 'tbl_10': tbl_10, 'tbl_11': tbl_11, 'tbl_12': tbl_12, 'tbl_13': tbl_13, 'tbl_14': tbl_14, 'tbl_15': tbl_15, 'tbl_16': tbl_16, 'tbl_17': tbl_17, 'tbl_18': tbl_18, 'tbl_19': tbl_19, 'tbl_20': tbl_20, 'tbl_21': tbl_21, 'tbl_22': tbl_22, 'tbl_23': tbl_23, 'tbl_24': tbl_24, 'tbl_25': tbl_25, 'tbl_26': tbl_26, 'tbl_27': tbl_27, 'tbl_28': tbl_28, 'tbl_29': tbl_29, 'tbl_30': tbl_30, 'tbl_31': tbl_31, 'tbl_32': tbl_32, 'tbl_33': tbl_33, 'tbl_34': tbl_34, 'tbl_35': tbl_35, 'tbl_36': tbl_36, 'tbl_37': tbl_37, 'tbl_38': tbl_38, 'W_top1': W_top1, 'b_top1': b_top1, 'W_top2': W_top2, 'b_top2': b_top2, 'W_top3': W_top3, 'L0_rec_W0': _L0_rec_in['W0'], 'L0_rec_b0': _L0_rec_in['b0'], 'L0_rec_W1': _L0_rec_in['W1'], 'L0_rec_b1': _L0_rec_in['b1'], 'L0_rec_W2': _L0_rec_in['W2'], 'L0_rec_b2': _L0_rec_in['b2']}

def reference(dense_ctx, ids, tbl_0, tbl_1, tbl_2, tbl_3, tbl_4, tbl_5, tbl_6, tbl_7, tbl_8, tbl_9, tbl_10, tbl_11, tbl_12, tbl_13, tbl_14, tbl_15, tbl_16, tbl_17, tbl_18, tbl_19, tbl_20, tbl_21, tbl_22, tbl_23, tbl_24, tbl_25, tbl_26, tbl_27, tbl_28, tbl_29, tbl_30, tbl_31, tbl_32, tbl_33, tbl_34, tbl_35, tbl_36, tbl_37, tbl_38, W_top1, b_top1, W_top2, b_top2, W_top3, L0_rec_W0, L0_rec_b0, L0_rec_W1, L0_rec_b1, L0_rec_W2, L0_rec_b2):
    import jax
    import jax.numpy as jnp

    def _L0_rec_ref(embedded_features, W0, b0, W1, b1, W2, b2):
        import jax, jax.numpy as jnp
        import numpy as np
        B, F0, D = (512, 39, 16)
        CIN = [128, 128, 128]

        def _cin_layer(X0, Xi, W, b):
            H = W.shape[0]
            F0_, Fi = (X0.shape[1], Xi.shape[1])
            Wr = W.reshape(H, F0_, Fi)
            return jnp.einsum('hjk,bjd,bkd->bhd', Wr, X0, Xi) + b[None, :, None]
        X0 = embedded_features
        Ws = [(W0, b0), (W1, b1), (W2, b2)]
        Xi = X0
        res = []
        for W, b in Ws:
            Xi = _cin_layer(X0, Xi, W, b)
            res.append(Xi.sum(axis=2))
        return jnp.concatenate(res, axis=1)
    e = jnp.stack([tbl_0[ids[:, 0]], tbl_1[ids[:, 1]], tbl_2[ids[:, 2]], tbl_3[ids[:, 3]], tbl_4[ids[:, 4]], tbl_5[ids[:, 5]], tbl_6[ids[:, 6]], tbl_7[ids[:, 7]], tbl_8[ids[:, 8]], tbl_9[ids[:, 9]], tbl_10[ids[:, 10]], tbl_11[ids[:, 11]], tbl_12[ids[:, 12]], tbl_13[ids[:, 13]], tbl_14[ids[:, 14]], tbl_15[ids[:, 15]], tbl_16[ids[:, 16]], tbl_17[ids[:, 17]], tbl_18[ids[:, 18]], tbl_19[ids[:, 19]], tbl_20[ids[:, 20]], tbl_21[ids[:, 21]], tbl_22[ids[:, 22]], tbl_23[ids[:, 23]], tbl_24[ids[:, 24]], tbl_25[ids[:, 25]], tbl_26[ids[:, 26]], tbl_27[ids[:, 27]], tbl_28[ids[:, 28]], tbl_29[ids[:, 29]], tbl_30[ids[:, 30]], tbl_31[ids[:, 31]], tbl_32[ids[:, 32]], tbl_33[ids[:, 33]], tbl_34[ids[:, 34]], tbl_35[ids[:, 35]], tbl_36[ids[:, 36]], tbl_37[ids[:, 37]], tbl_38[ids[:, 38]]], axis=1)
    z = _L0_rec_ref(e, L0_rec_W0, L0_rec_b0, L0_rec_W1, L0_rec_b1, L0_rec_W2, L0_rec_b2)
    z = z.reshape(z.shape[0], -1)
    h = jnp.concatenate([z, dense_ctx], axis=1)
    h = jnp.maximum(h @ W_top1 + b_top1, 0.0)
    h = jnp.maximum(h @ W_top2 + b_top2, 0.0)
    y = h @ W_top3
    return y

_drawn_inputs = setup_inputs


def setup_inputs(seed=0):
    import zlib

    import numpy as np

    out = dict(_drawn_inputs(seed))
    spreads = {'b_top1': (0.0, 0.1),
     'b_top2': (0.0, 0.1),
     'L0_rec_b0': (0.0, 0.1),
     'L0_rec_b1': (0.0, 0.1),
     'L0_rec_b2': (0.0, 0.1)}
    factors = {'tbl_0': 8.0,
     'tbl_1': 6.311,
     'tbl_2': 5.347,
     'tbl_3': 7.092,
     'tbl_4': 8.0,
     'tbl_5': 8.0,
     'tbl_6': 8.0,
     'tbl_7': 6.921,
     'tbl_8': 8.0,
     'tbl_9': 8.0,
     'tbl_10': 8.0,
     'tbl_11': 6.361,
     'tbl_12': 8.0,
     'tbl_13': 8.0,
     'tbl_14': 4.308,
     'tbl_15': 5.997,
     'tbl_16': 8.0,
     'tbl_17': 8.0,
     'tbl_18': 8.0,
     'tbl_19': 6.028,
     'tbl_20': 7.17,
     'tbl_21': 8.0,
     'tbl_22': 8.0,
     'tbl_23': 8.0,
     'tbl_24': 8.0,
     'tbl_25': 7.184,
     'tbl_26': 5.78,
     'tbl_27': 8.0,
     'tbl_28': 8.0,
     'tbl_29': 8.0,
     'tbl_30': 6.985,
     'tbl_31': 6.124,
     'tbl_32': 8.0,
     'tbl_33': 6.159,
     'tbl_34': 8.0,
     'tbl_35': 7.858,
     'tbl_36': 8.0,
     'tbl_37': 6.918,
     'tbl_38': 8.0,
     'L0_rec_W0': 3.079}
    for name, (base, spread) in spreads.items():
        noise = np.random.default_rng([zlib.crc32(name.encode()), seed]).standard_normal(out[name].shape)
        drawn = base * np.exp(spread * noise) if base else spread * noise
        out[name] = jnp.asarray(drawn.astype(out[name].dtype))
    for name, factor in factors.items():
        out[name] = (out[name] * factor).astype(out[name].dtype)
    return out
```

```python
from contextlib import ExitStack

import concourse.bass as bass
from concourse import mybir

B, F, D, H = 512, 39, 16, 128
P = 128
COLS = 512
TILES_PER_GROUP = COLS // P
GROUPS = B * D // COLS
TILES = GROUPS * TILES_PER_GROUP
GB = COLS // D
TB = P // D
QUARTERS = B // P
FD = F * D
J1 = F + 1
SHIFTS = F // 2 + 1
PER_BLOCK = P // F
BLOCKS = -(-SHIFTS // PER_BLOCK)
ROWS = [F * min(PER_BLOCK, SHIFTS - PER_BLOCK * b) for b in range(BLOCKS)]
PAIRS = PER_BLOCK * F
LO = 64
STACK = LO + F
UNITS = COLS // H
CHUNKS = -(-F // UNITS)
WIDTH = [min(UNITS, F - UNITS * c) for c in range(CHUNKS)]
T_BANKS = 5
ACT_CHUNKS = [0, 1, 3, 4, 6, 7, 9]
DVE_CHUNKS = [c for c in range(CHUNKS) if c not in ACT_CHUNKS]
NA, ND = len(ACT_CHUNKS), len(DVE_CHUNKS)
RED = 4
HR = H // RED
X0_COPIES = 5
W2_SLOT = 5
W2_LOADS = -(-F // W2_SLOT)
W2_SLOTS = 3
PIECES = [(0, 2), (2, 3), (3, 4)]
TOP1, TOP2 = 512, 256
M1, M2 = TOP1 // P, TOP2 // P
SEL_AT = [8 + 3 * b for b in range(BLOCKS)]
PAIR_AT = [11 + 3 * b for b in range(BLOCKS)]


def tower_program(nc, ids, tables, dense_t, pair_a, pair_b, w1, w2, b0, b1, b2,
                  top1, top_b1, top2, top_b2, top3, select, consts, out):
    f32, f32r, i32 = mybir.dt.float32, mybir.dt.float32r, mybir.dt.int32
    ALU = mybir.AluOpType
    ACT = mybir.ActivationFunctionType
    AX = mybir.AxisListType
    ctx = ExitStack()
    with ctx:
        def sb(name, shape, dt=f32):
            return ctx.enter_context(nc.sbuf_tensor(name, shape, dt))

        def pb(name, shape):
            return ctx.enter_context(nc.psum_tensor(name, shape, f32))

        def sem(name):
            return ctx.enter_context(nc.semaphore(name))

        idx = sb("idx", [P, QUARTERS * F], i32)
        emb = sb("emb", [P, 2, FD])
        emb_dram = nc.dram_tensor("emb_scratch", (B, FD), f32, kind="Internal").ap()
        rep = sb("rep", [PAIRS, COLS])
        raw = sb("raw", [STACK, COLS])
        stack = sb("stack", [STACK, COLS], f32r)
        x0t = sb("x0t", [P, TILES_PER_GROUP, J1])
        diag = sb("diag", [P, 2, TB, J1])
        pairs = sb("pairs", [PAIRS, 2, COLS])
        x1 = sb("x1", [P, COLS])
        x1_hi = sb("x1_hi", [P, COLS], f32r)
        x1_lo = sb("x1_lo", [P, COLS], f32r)
        prod = sb("prod", [P, 2, J1, H])
        x2 = sb("x2", [P, 2, H])
        G = sb("G", [P, J1, B])
        w1_hi = sb("w1_hi", [P, F * H], f32r)
        w1_lo = sb("w1_lo", [P, F * H], f32r)
        w2_ring = sb("w2_ring", [P, W2_SLOTS, W2_SLOT * H])
        w_pair = sb("w_pair", [PAIRS, BLOCKS, H])
        sel = sb("sel", [STACK, BLOCKS * PAIRS + J1], f32r)
        mask = sb("mask", [P, TB])
        z0 = sb("z0", [P, B])
        z2 = sb("z2", [P, B])
        dense = sb("dense", [D, B])
        bias = sb("bias", [P, 2 + M1 + M2])
        bias16 = sb("bias16", [P, 1])
        w3 = sb("w3", [P, M2])
        y = sb("y", [1, B])
        flat_g = G[:, :, :].rearrange("p j b -> p (j b)")
        w1_raw = flat_g[:, 0:F * H]
        at = F * H
        pair_a_raw = flat_g[0:PAIRS, at:at + BLOCKS * H]
        at += BLOCKS * H
        pair_b_raw = flat_g[0:PAIRS, at:at + BLOCKS * H]
        at += BLOCKS * H
        sel_raw = flat_g[0:STACK, at:at + BLOCKS * PAIRS + J1]
        flat_p = prod[:, :, :, :].rearrange("p a j h -> p (a j h)")
        wt1 = flat_p[:, 0:4 * TOP1].rearrange("p (c n) -> p c n", c=4)
        wt2 = flat_p[:, 4 * TOP1:4 * TOP1 + M1 * TOP2].rearrange("p (c n) -> p c n", c=M1)
        at = 4 * TOP1 + M1 * TOP2
        h1 = flat_p[:, at:at + M1 * B].rearrange("p (c n) -> p c n", c=M1)
        at += M1 * B
        h2 = flat_p[:, at:at + M2 * B].rearrange("p (c n) -> p c n", c=M2)

        t_bank = [pb(f"t_bank{i}", [P, COLS]) for i in range(T_BANKS)]
        sel_bank = pb("sel_bank", [P, COLS])
        x1_bank = pb("x1_bank", [P, COLS])
        small_bank = pb("small_bank", [P, COLS])
        g_psum = small_bank[:, 0:TB * J1].rearrange("p (b j) -> p b j", b=TB)
        x0t_psum = small_bank[:, TB * J1:TB * J1 + J1]

        ids_loaded = sem("ids_loaded")
        w_loaded = sem("w_loaded")
        small_loaded = sem("small_loaded")
        raw_zeroed = sem("raw_zeroed")
        ones_set = sem("ones_set")
        bias16_ready = sem("bias16_ready")
        gathered = [sem(f"gathered{q}") for q in range(QUARTERS)]
        emb_stored = [sem(f"emb_stored{q}") for q in range(QUARTERS)]
        w_split_hi = sem("w_split_hi")
        w_split_lo = sem("w_split_lo")
        sel_ready = sem("sel_ready")
        wpair_ready = sem("wpair_ready")
        x0_loaded = sem("x0_loaded")
        stack_hi = sem("stack_hi")
        stack_lo = sem("stack_lo")
        x0t_mm = sem("x0t_mm")
        x0t_ready = sem("x0t_ready")
        sel_mm = sem("sel_mm")
        pair_ready = sem("pair_ready")
        pair_mm = sem("pair_mm")
        x1_ready = sem("x1_ready")
        x1_hi_ready = sem("x1_hi_ready")
        x1_lo_ready = sem("x1_lo_ready")
        z0_ready = sem("z0_ready")
        t_mm = sem("t_mm")
        act_scaled = sem("act_scaled")
        dve_scaled = sem("dve_scaled")
        summed = sem("summed")
        diag_ready = sem("diag_ready")
        g_mm = sem("g_mm")
        g_copied = sem("g_copied")
        w2_loaded = [sem(f"w2_loaded{i}") for i in range(W2_SLOTS)]
        w2_used = sem("w2_used")
        z2_ready = sem("z2_ready")
        top_loaded = sem("top_loaded")
        top_mm = sem("top_mm")
        h_ready = sem("h_ready")
        y_ready = sem("y_ready")
        y_stored = sem("y_stored")
        block = ctx.enter_context(nc.Block())

        def scaled_before(t, c):
            tile, chunk = (t, c - T_BANKS) if c >= T_BANKS else (t - 1, c - T_BANKS + CHUNKS)
            if chunk in ACT_CHUNKS:
                return act_scaled, tile * NA + (ACT_CHUNKS.index(chunk) + 1)
            return dve_scaled, tile * ND + (DVE_CHUNKS.index(chunk) + 1)

        @block.sync
        def _(sp):
            sp.dma_start(idx[:, :].rearrange("p (q f) -> p q f", q=QUARTERS),
                         ids.rearrange("(q p) f -> p q f", p=P)).then_inc(ids_loaded, 16)
            sp.dma_start(sel_raw, select).then_inc(w_loaded, 16)
            sp.dma_start(pair_a_raw, pair_a).then_inc(w_loaded, 16)
            sp.dma_start(pair_b_raw, pair_b).then_inc(w_loaded, 16)
            sp.dma_start(w1_raw, w1).then_inc(w_loaded, 16)
            for slot in range(2):
                sp.dma_start(prod[:, slot, F, :], b1.to_broadcast([P, H])).then_inc(small_loaded, 16)
            sp.dma_start(mask[:, :], consts).then_inc(small_loaded, 16)
            sp.dma_start(bias[:, 0:1], b0).then_inc(small_loaded, 16)
            sp.dma_start(bias[:, 1:2], b2).then_inc(small_loaded, 16)
            sp.dma_start(bias[:, 2:2 + M1], top_b1).then_inc(small_loaded, 16)
            sp.dma_start(bias[:, 2 + M1:], top_b2).then_inc(small_loaded, 16)
            sp.dma_start(w3[:, :], top3).then_inc(small_loaded, 16)
            sp.dma_start(dense[:, :], dense_t).then_inc(small_loaded, 16)
            for i in range(W2_SLOTS):
                sp.dma_start(w2_ring[:, i, :], w2[:, i * W2_SLOT * H:(i + 1) * W2_SLOT * H]).then_inc(w2_loaded[i], 16)
            sp.wait_ge(raw_zeroed, 1)

            def load_x0(g):
                src = emb_dram[bass.ds(g * GB, GB), :].rearrange("b (f d) -> f b d", d=D)
                for dst, row in ((rep, 0), (rep, F), (rep, 2 * F), (raw, 0), (raw, LO)):
                    sp.dma_start(dst[row:row + F, :].rearrange("f (b d) -> f b d", d=D), src).then_inc(x0_loaded, 16)

            for q in range(QUARTERS):
                sp.wait_ge(emb_stored[q], 16)
                if q == 0:
                    load_x0(0)
                with sp.Fori(max(q * GROUPS // QUARTERS, 1), (q + 1) * GROUPS // QUARTERS) as g:
                    sp.wait_ge(pair_ready, g * BLOCKS)
                    sp.wait_ge(stack_lo, g)
                    load_x0(g)
            sp.wait_ge(summed, TILES * RED)
            for c in range(3):
                sp.dma_start(wt1[:, c, :], top1[c * P:(c + 1) * P, :]).then_inc(top_loaded, 16)
            sp.dma_start(wt1[0:D, 3, :], top1[3 * P:3 * P + D, :]).then_inc(top_loaded, 16)
            sp.dma_start(wt2, top2.rearrange("(c p) n -> p c n", p=P)).then_inc(top_loaded, 16)
            for i in range(W2_SLOTS, W2_LOADS):
                n = min(W2_SLOT, F - i * W2_SLOT)
                sp.wait_ge(w2_used, i - W2_SLOTS + 1)
                sp.dma_start(w2_ring[:, i % W2_SLOTS, 0:n * H],
                             w2[:, i * W2_SLOT * H:(i * W2_SLOT + n) * H]).then_inc(w2_loaded[i % W2_SLOTS], 16)
            sp.wait_ge(y_ready, 1)
            sp.dma_start(out.rearrange("b o -> o b"), y[:, :]).then_inc(y_stored, 16)
            sp.wait_ge(y_stored, 16)

        @block.gpsimd
        def _(pool):
            pool.memset(raw[:, :], 0.0).then_inc(raw_zeroed, 1)
            pool.memset(x0t[:, :, :], 1.0).then_inc(ones_set, 1)
            pool.wait_ge(ids_loaded, 16)

            def gather(q, f):
                if q >= 2 and f == 0:
                    pool.wait_ge(emb_stored[q - 2], 16)
                pool.indirect_dma_start(
                    out=emb[:, q % 2, f * D:(f + 1) * D], out_offset=None, in_=tables[f],
                    in_offset=bass.IndirectOffsetOnAxis(ap=idx[:, q * F + f:q * F + f + 1], axis=0),
                ).then_inc(gathered[q], 16)

            def store(q):
                pool.wait_ge(gathered[q], 16 * F)
                pool.dma_start(emb_dram[q * P:(q + 1) * P, :], emb[:, q % 2, :]).then_inc(emb_stored[q], 16)

            def diagonal(t, slot, first):
                pool.wait_ge(x0t_ready, t + 1)
                if not first:
                    pool.wait_ge(g_mm, t - 1)
                pool.tensor_tensor(
                    diag[:, slot % 2, :, :],
                    x0t[:, slot:slot + 1, :].to_broadcast([P, TB, J1]),
                    mask[:, :].unsqueeze(2).to_broadcast([P, TB, J1]), ALU.mult).then_inc(diag_ready, 1)

            for f in range(F):
                gather(0, f)
            store(0)
            pool.wait_ge(small_loaded, 16 * 9)
            per_quarter = TILES // QUARTERS
            share = -(-F // (per_quarter - 1))
            for q in range(QUARTERS - 1):
                for i in range(per_quarter):
                    for f in range(i * share, min((i + 1) * share, F)):
                        gather(q + 1, f)
                    if i * share < F <= (i + 1) * share:
                        store(q + 1)
                    t = q * per_quarter + i
                    diagonal(t, t % TILES_PER_GROUP, t < 2)
            with pool.Fori(GROUPS - GROUPS // QUARTERS, GROUPS) as g:
                for s in range(TILES_PER_GROUP):
                    diagonal(g * TILES_PER_GROUP + s, s, False)

        @block.tensor
        def _(pe):
            def select_pairs(g, b):
                if b == 0:
                    pe.wait_ge(stack_lo, g + 1)
                if not (b == 0 and isinstance(g, int) and g == 0):
                    pe.wait_ge(pair_ready, g * BLOCKS + b)
                pe.matmul(sel_bank[0:ROWS[b], :], sel[:, b * PAIRS:b * PAIRS + ROWS[b]], stack[:, :],
                          start=True, stop=True).then_inc(sel_mm, 1)

            def pair_product(g, b):
                pe.wait_ge(pair_ready, g * BLOCKS + (b + 1))
                if b == 0 and not (isinstance(g, int) and g == 0):
                    pe.wait_ge(x1_ready, g)
                pe.matmul(x1_bank[:, :], w_pair[0:ROWS[b], b, :], pairs[0:ROWS[b], b % 2, :],
                          start=b == 0, stop=b == BLOCKS - 1).then_inc(pair_mm, 1)

            def transpose_x0(g, s, copied=None):
                if s == 0:
                    pe.wait_ge(stack_lo, g + 1)
                if not (s == 0 and isinstance(g, int) and g == 0):
                    pe.wait_ge(x0t_ready, g * TILES_PER_GROUP + s)
                if copied is not None:
                    pe.wait_ge(g_copied, copied)
                pe.matmul(x0t_psum, stack[:, s * P:(s + 1) * P], sel[:, BLOCKS * PAIRS:],
                          start=True, stop=True).then_inc(x0t_mm, 1)

            def g_product(t, slot, transposed):
                pe.wait_ge(summed, (t + 1) * RED)
                pe.wait_ge(diag_ready, t + 1)
                pe.wait_ge(x0t_ready, transposed)
                if not (isinstance(t, int) and t == 0):
                    pe.wait_ge(g_copied, t)
                pe.matmul(small_bank[:, 0:TB * J1], x2[:, slot % 2, :],
                          diag[:, slot % 2, :, :].rearrange("p b j -> p (b j)"),
                          start=True, stop=True).then_inc(g_mm, 1)

            def t_chunk(t, s, c, first_tile):
                if not (first_tile and c < T_BANKS):
                    pe.wait_ge(*scaled_before(t, c))
                cols = slice(c * COLS, c * COLS + WIDTH[c] * H)
                acc = t_bank[c % T_BANKS][:, 0:WIDTH[c] * H]
                hi, lo = x1_hi[:, s * P:(s + 1) * P], x1_lo[:, s * P:(s + 1) * P]
                pe.matmul(acc, hi, w1_hi[:, cols], start=True, stop=False)
                pe.matmul(acc, hi, w1_lo[:, cols], start=False, stop=False)
                pe.matmul(acc, lo, w1_hi[:, cols], start=False, stop=True).then_inc(t_mm, 1)

            def group(g, first=False, last=False):
                for s in range(TILES_PER_GROUP):
                    t = g * TILES_PER_GROUP + s
                    piece = 0 if s < 2 else s - 1
                    pe.wait_ge(x1_lo_ready, g * len(PIECES) + (piece + 1))
                    for c in range(CHUNKS):
                        p = s * CHUNKS + c
                        t_chunk(t, s, c, first and s == 0)
                        if p == 2:
                            transpose_x0(g, TILES_PER_GROUP - 1, None if first else t - 2)
                        if c == 5 and not (first and s < 2):
                            ahead = 0 if last else max(s - 1, 0)
                            g_product(t - 2, s, (g + 1) * TILES_PER_GROUP + ahead)
                        if not last:
                            if c == 8 and s > 0:
                                transpose_x0(g + 1, s - 1, None if first and s < 2 else t - 1)
                            if p in SEL_AT:
                                select_pairs(g + 1, SEL_AT.index(p))
                            if p in PAIR_AT:
                                pair_product(g + 1, PAIR_AT.index(p))

            pe.wait_ge(sel_ready, 1)
            pe.wait_ge(wpair_ready, 1)
            for b in range(BLOCKS):
                select_pairs(0, b)
                if b < TILES_PER_GROUP - 1:
                    transpose_x0(0, b)
                if b > 0:
                    pair_product(0, b - 1)
            pair_product(0, BLOCKS - 1)
            pe.wait_ge(w_split_lo, 1)
            group(0, first=True)
            with pe.Fori(1, GROUPS - 1) as g:
                group(g)
            group(GROUPS - 1, last=True)
            g_product(TILES - 2, 0, TILES)
            g_product(TILES - 1, 1, TILES)

            pe.wait_ge(g_copied, TILES)
            for j in range(F):
                i, k = j // W2_SLOT, j % W2_SLOT
                if k == 0:
                    pe.wait_ge(w2_loaded[i % W2_SLOTS], 16 * (i // W2_SLOTS + 1))
                mm = pe.matmul(t_bank[0][:, :], w2_ring[:, i % W2_SLOTS, k * H:(k + 1) * H], G[:, j, :],
                               start=j == 0, stop=j == F - 1)
                if k == W2_SLOT - 1 or j == F - 1:
                    mm.then_inc(w2_used, 1)

            pe.wait_ge(top_loaded, 16 * 5)
            pe.wait_ge(z0_ready, GROUPS)
            feats = [z0[:, :], G[:, F, :], dense[:, :], z2[:, :]]
            weights = [(0, P), (1, P), (3, D), (2, P)]
            for m in range(M1):
                for n in range(3):
                    w, k = weights[n]
                    pe.matmul(t_bank[1 + m][:, :], wt1[0:k, w, m * P:(m + 1) * P], feats[n],
                              start=n == 0, stop=False)
            pe.wait_ge(z2_ready, 1)
            for m in range(M1):
                pe.matmul(t_bank[1 + m][:, :], wt1[:, 2, m * P:(m + 1) * P], feats[3],
                          start=False, stop=True).then_inc(top_mm, 1)
            for m in range(M2):
                for c in range(M1):
                    pe.wait_ge(h_ready, c + 1)
                    mm = pe.matmul((sel_bank, x1_bank)[m][:, :], wt2[:, c, m * P:(m + 1) * P], h1[:, c, :],
                                   start=c == 0, stop=c == M1 - 1)
                mm.then_inc(top_mm, 1)
            for m in range(M2):
                pe.wait_ge(h_ready, M1 + m + 1)
                mm = pe.matmul(small_bank[0:1, :], w3[:, m:m + 1], h2[:, m, :], start=m == 0, stop=m == M2 - 1)
            mm.then_inc(top_mm, 1)

        @block.scalar
        def _(act):
            def copy_x0t(g, s, first):
                t = g * TILES_PER_GROUP + s
                act.wait_ge(x0t_mm, t + 1)
                if not first:
                    prev = t - TILES_PER_GROUP
                    act.wait_ge(act_scaled, (prev + 1) * NA)
                    act.wait_ge(dve_scaled, (prev + 1) * ND)
                    act.wait_ge(diag_ready, prev + 1)
                act.activation(x0t[:, s, 0:F], x0t_psum[:, 0:F], ACT.Copy).then_inc(x0t_ready, 1)

            def split_x0_hi(g, first):
                act.wait_ge(x0_loaded, (g + 1) * (16 * X0_COPIES))
                if not first:
                    act.wait_ge(x0t_mm, g * TILES_PER_GROUP)
                    act.wait_ge(sel_mm, g * BLOCKS)
                act.activation(stack[:, :], raw[:, :], ACT.Copy).then_inc(stack_hi, 1)

            def bias_x1(g, first):
                act.wait_ge(pair_mm, (g + 1) * BLOCKS)
                if not first:
                    act.wait_ge(x1_lo_ready, g * len(PIECES))
                    act.wait_ge(z0_ready, g)
                act.activation(x1[:, :], x1_bank[:, :], ACT.Identity, bias=bias[:, 0:1]).then_inc(x1_ready, 1)

            def split_x1_hi(g, i, first):
                a, b = PIECES[i]
                act.wait_ge(x1_ready, g + 1)
                if not first:
                    act.wait_ge(t_mm, (g - 1) * (TILES_PER_GROUP * CHUNKS) + b * CHUNKS)
                act.activation(x1_hi[:, a * P:b * P], x1[:, a * P:b * P], ACT.Copy).then_inc(x1_hi_ready, 1)

            def copy_g(t, g, s):
                act.wait_ge(g_mm, t + 1)
                act.activation(G[:, :, bass.ds(g * GB + s * TB, TB)].rearrange("p j b -> p b j"),
                               g_psum, ACT.Copy).then_inc(g_copied, 1)

            def scale_chunk(t, s, c, first):
                act.wait_ge(t_mm, t * CHUNKS + (c + 1))
                if c == ACT_CHUNKS[0]:
                    act.wait_ge(x0t_ready, t + 1)
                    if not (first and s < 2):
                        act.wait_ge(summed, (t - 1) * RED)
                for u in range(WIDTH[c]):
                    j = c * UNITS + u
                    last = act.activation(prod[:, s % 2, j, :], t_bank[c % T_BANKS][:, u * H:(u + 1) * H],
                                          ACT.Copy, scale=x0t[:, s, j:j + 1])
                last.then_inc(act_scaled, 1)

            def group(g, first=False, last=False):
                for s in range(TILES_PER_GROUP):
                    t = g * TILES_PER_GROUP + s
                    for c in ACT_CHUNKS:
                        scale_chunk(t, s, c, first)
                        if s == 0 and c == 0:
                            split_x1_hi(g, 2, first)
                        if s == 0 and c == 3:
                            copy_x0t(g, TILES_PER_GROUP - 1, first)
                        if c == 6 and not (first and s < 2):
                            copy_g(t - 2, g if s >= 2 else g - 1, (s - 2) % TILES_PER_GROUP)
                        if not last:
                            if s == 0 and c == 4:
                                split_x0_hi(g + 1, False)
                            if s > 0 and c == 9:
                                copy_x0t(g + 1, s - 1, False)
                            if s == 3 and c == 0:
                                bias_x1(g + 1, False)
                                split_x1_hi(g + 1, 0, False)
                            if s == 3 and c == 1:
                                split_x1_hi(g + 1, 1, False)

            act.wait_ge(w_loaded, 16 * 4)
            act.activation(sel[:, :], sel_raw, ACT.Copy).then_inc(sel_ready, 1)
            act.activation(w1_hi[:, :], w1_raw, ACT.Copy).then_inc(w_split_hi, 1)
            act.wait_ge(ones_set, 1)
            act.wait_ge(small_loaded, 16 * 9)
            split_x0_hi(0, True)
            for s in range(TILES_PER_GROUP - 1):
                copy_x0t(0, s, True)
            bias_x1(0, True)
            split_x1_hi(0, 0, True)
            split_x1_hi(0, 1, True)
            group(0, first=True)
            with act.Fori(1, GROUPS - 1) as g:
                group(g)
            group(GROUPS - 1, last=True)
            copy_g(TILES - 2, GROUPS - 1, 2)
            copy_g(TILES - 1, GROUPS - 1, 3)
            act.wait_ge(bias16_ready, 1)
            act.wait_ge(w2_used, W2_LOADS)
            act.activation(z2[:, :], t_bank[0][:, :], ACT.Identity, bias=bias16[:, 0:1]).then_inc(z2_ready, 1)
            for m in range(M1):
                act.wait_ge(top_mm, m + 1)
                act.activation(h1[:, m, :], t_bank[1 + m][:, :], ACT.Relu, bias=bias[:, 2 + m:3 + m]).then_inc(h_ready, 1)
            for m in range(M2):
                act.wait_ge(top_mm, M1 + m + 1)
                act.activation(h2[:, m, :], (sel_bank, x1_bank)[m][:, :], ACT.Relu,
                               bias=bias[:, 2 + M1 + m:3 + M1 + m]).then_inc(h_ready, 1)
            act.wait_ge(top_mm, M1 + M2 + 1)
            act.activation(y[:, :], small_bank[0:1, :], ACT.Copy).then_inc(y_ready, 1)

        @block.vector
        def _(dve):
            def split_x0_lo(g):
                dve.wait_ge(stack_hi, g + 1)
                dve.tensor_tensor(stack[LO:STACK, :], raw[LO:STACK, :], stack[LO:STACK, :],
                                  ALU.subtract).then_inc(stack_lo, 1)

            def form_pairs(g, b, first):
                dve.wait_ge(sel_mm, g * BLOCKS + (b + 1))
                if not (first and b < 2):
                    dve.wait_ge(pair_mm, g * BLOCKS + max(b - 1, 0))
                dve.tensor_tensor(pairs[0:ROWS[b], b % 2, :], sel_bank[0:ROWS[b], :], rep[0:ROWS[b], :],
                                  ALU.mult).then_inc(pair_ready, 1)

            def split_x1_lo(g, i):
                a, b = PIECES[i]
                dve.wait_ge(x1_hi_ready, g * len(PIECES) + (i + 1))
                dve.tensor_tensor(x1_lo[:, a * P:b * P], x1[:, a * P:b * P], x1_hi[:, a * P:b * P],
                                  ALU.subtract).then_inc(x1_lo_ready, 1)

            def sum_z0(g):
                dve.wait_ge(x1_ready, g + 1)
                dve.tensor_reduce(z0[:, bass.ds(g * GB, GB)],
                                  x1[:, :].rearrange("p (b d) -> p b d", d=D), AX.X, ALU.add)\
                   .then_inc(z0_ready, 1)

            def scale_chunk(t, s, c, first):
                dve.wait_ge(t_mm, t * CHUNKS + (c + 1))
                if c == DVE_CHUNKS[0]:
                    dve.wait_ge(x0t_ready, t + 1)
                    if not (first and s < 2):
                        dve.wait_ge(summed, (t - 1) * RED)
                j, n = c * UNITS, WIDTH[c]
                dve.tensor_tensor(prod[:, s % 2, j:j + n, :],
                                  t_bank[c % T_BANKS][:, 0:n * H].rearrange("p (j h) -> p j h", h=H),
                                  x0t[:, s, j:j + n].unsqueeze(2).to_broadcast([P, n, H]),
                                  ALU.mult).then_inc(dve_scaled, 1)

            def sum_over_j(t, slot, i, first):
                if i == 0:
                    dve.wait_ge(act_scaled, (t + 1) * NA)
                    dve.wait_ge(dve_scaled, (t + 1) * ND)
                    if not first:
                        dve.wait_ge(g_mm, t - 1)
                h = slice(i * HR, (i + 1) * HR)
                dve.tensor_reduce(x2[:, slot % 2, h], prod[:, slot % 2, :, h].rearrange("p j h -> p h j"),
                                  AX.X, ALU.add).then_inc(summed, 1)

            def group(g, first=False, last=False):
                for s in range(TILES_PER_GROUP):
                    t = g * TILES_PER_GROUP + s
                    for c in range(CHUNKS):
                        p = s * CHUNKS + c
                        if c in DVE_CHUNKS:
                            scale_chunk(t, s, c, first)
                        if not last:
                            if p in SEL_AT:
                                form_pairs(g + 1, SEL_AT.index(p), False)
                            if p == 5:
                                split_x0_lo(g + 1)
                            if p == 32:
                                split_x1_lo(g + 1, 0)
                            if p == 33:
                                split_x1_lo(g + 1, 1)
                            if p == 35:
                                sum_z0(g + 1)
                        if p == 2:
                            split_x1_lo(g, 2)
                        if c in (3, 5, 6, 8) and not (first and s == 0):
                            sum_over_j(t - 1, s + 1, (3, 5, 6, 8).index(c), first and s < 3)

            dve.wait_ge(w_loaded, 16 * 4)
            dve.tensor_tensor(w_pair[:, :, :].rearrange("p c h -> p (c h)"), pair_a_raw, pair_b_raw,
                              ALU.add).then_inc(wpair_ready, 1)
            dve.wait_ge(w_split_hi, 1)
            dve.tensor_tensor(w1_lo[:, :], w1_raw, w1_hi[:, :], ALU.subtract).then_inc(w_split_lo, 1)
            dve.wait_ge(small_loaded, 16 * 9)
            dve.tensor_scalar(bias16[:, :], bias[:, 1:2], float(D), None, ALU.mult).then_inc(bias16_ready, 1)
            split_x0_lo(0)
            for b in range(BLOCKS):
                form_pairs(0, b, True)
            split_x1_lo(0, 0)
            split_x1_lo(0, 1)
            sum_z0(0)
            group(0, first=True)
            with dve.Fori(1, GROUPS - 1) as g:
                group(g)
            group(GROUPS - 1, last=True)
            for i in range(RED):
                sum_over_j(TILES - 1, 1, i, False)


def kernel(**inputs):
    import numpy as np
    import concourse.bacc as _bacc
    from concourse.bass_utils import run_bass_kernel_spmd as _run

    w0 = np.asarray(inputs["L0_rec_W0"]).reshape(H, F, F)
    zero = np.zeros((F, H), w0.dtype)

    def shifted(w, first):
        wide = np.concatenate([w, w], axis=1).reshape(F * 2 * F, H)
        rows = [wide[s:s + (F - 1) * (2 * F + 1) + 1:2 * F + 1] for s in range(SHIFTS)]
        if not first:
            rows[0] = zero
        rows += [zero] * (BLOCKS * PER_BLOCK - SHIFTS)
        return np.ascontiguousarray(np.stack(rows).reshape(BLOCKS, PAIRS, H).transpose(1, 0, 2)).reshape(PAIRS, BLOCKS * H)

    def by_k(w):
        return np.ascontiguousarray(np.asarray(w).reshape(H, F, H).transpose(2, 1, 0)).reshape(H, F * H)

    select = np.zeros((STACK, BLOCKS * PAIRS + J1), np.float32)
    for row in (0, LO):
        for s in range(SHIFTS):
            for j in range(F):
                select[row + (j + s) % F, s * F + j] = 1.0
        for j in range(F):
            select[row + j, BLOCKS * PAIRS + j] = 1.0
    same = np.zeros((P, TB), np.float32)
    for p in range(P):
        same[p, p // D] = 1.0

    arrays = {
        "ids": np.ascontiguousarray(inputs["ids"]),
        "dense_t": np.ascontiguousarray(np.asarray(inputs["dense_ctx"]).T),
        "pair_a": shifted(w0.transpose(1, 2, 0), True),
        "pair_b": shifted(w0.transpose(2, 1, 0), False),
        "w1": by_k(inputs["L0_rec_W1"]),
        "w2": by_k(inputs["L0_rec_W2"]),
        "b0": np.asarray(inputs["L0_rec_b0"]).reshape(H, 1),
        "b1": np.asarray(inputs["L0_rec_b1"]).reshape(1, H),
        "b2": np.asarray(inputs["L0_rec_b2"]).reshape(H, 1),
        "top1": np.ascontiguousarray(inputs["W_top1"]),
        "top_b1": np.ascontiguousarray(np.asarray(inputs["b_top1"]).reshape(M1, P).T),
        "top2": np.ascontiguousarray(inputs["W_top2"]),
        "top_b2": np.ascontiguousarray(np.asarray(inputs["b_top2"]).reshape(M2, P).T),
        "top3": np.ascontiguousarray(np.asarray(inputs["W_top3"]).reshape(M2, P).T),
        "select": select,
        "consts": same,
    }
    for f in range(F):
        arrays[f"tbl_{f}"] = np.ascontiguousarray(inputs[f"tbl_{f}"])

    nc = _bacc.Bacc("TRN2", target_bir_lowering=False, num_devices=1)
    aps = {n: nc.dram_tensor(f"in_{n}", a.shape, mybir.dt.from_np(a.dtype), kind="ExternalInput").ap()
           for n, a in arrays.items()}
    out = nc.dram_tensor("out_y", (B, 1), mybir.dt.float32, kind="ExternalOutput").ap()
    tables = [aps.pop(f"tbl_{f}") for f in range(F)]
    tower_program(nc, tables=tables, out=out, **aps)
    r = _run(nc, [{f"in_{n}": a for n, a in arrays.items()}], core_ids=[0])
    return r.results[0]["out_y"]
```

```python
from contextlib import ExitStack

import concourse.bass as bass
from concourse import mybir

B, F, D, H = 512, 39, 16, 128
P = 128
COLS = 512
TILES_PER_GROUP = COLS // P
GROUPS = B * D // COLS
TILES = GROUPS * TILES_PER_GROUP
GB = COLS // D
TB = P // D
QUARTERS = B // P
FD = F * D
J1 = F + 1
SHIFTS = F // 2 + 1
PER_BLOCK = P // F
BLOCKS = -(-SHIFTS // PER_BLOCK)
ROWS = [F * min(PER_BLOCK, SHIFTS - PER_BLOCK * b) for b in range(BLOCKS)]
PAIRS = PER_BLOCK * F
STACK = 2 * F
UNITS = COLS // H
CHUNKS = -(-F // UNITS)
WIDTH = [min(UNITS, F - UNITS * c) for c in range(CHUNKS)]
T_BANKS = 5
ACT_CHUNKS = [0, 1, 3, 5, 7, 9]
DVE_CHUNKS = [c for c in range(CHUNKS) if c not in ACT_CHUNKS]
NA, ND = len(ACT_CHUNKS), len(DVE_CHUNKS)
RED = 4
HR = H // RED
X0_COPIES = 3
W2_SLOT = 3
W2_LOADS = -(-F // W2_SLOT)
W2_SLOTS = 3
SMALL_LOADS = 8
TOP_LOADS = 6
PIECES = [(0, 3), (3, 4)]
FOLD = 8
TOP1, TOP2 = 512, 256
M1, M2 = TOP1 // P, TOP2 // P
SEL_AT = [5 + 4 * b for b in range(BLOCKS)]
PAIR_AT = [p + 4 for p in SEL_AT]
AHEAD = 15
GATHERS = (3, 2, 2, 3)
STORE_AT = 10
G_AT = 5
G_COPY_AT = 7
BIAS_AT = 5
X1_LO_AT = 37
Z0_AT = 39
SUM_AT = (1, 3, 5, 7)


def tower_program(nc, ids, tables, dense_t, pair_a, pair_b, w1, w2, b0, b1, b2,
                  top1, top_b1, top2, top_b2, top3, select, consts, out):
    f32, f32r, i32 = mybir.dt.float32, mybir.dt.float32r, mybir.dt.int32
    ALU = mybir.AluOpType
    ACT = mybir.ActivationFunctionType
    AX = mybir.AxisListType
    ctx = ExitStack()
    with ctx:
        def sb(name, shape, dt=f32):
            return ctx.enter_context(nc.sbuf_tensor(name, shape, dt))

        def pb(name, shape):
            return ctx.enter_context(nc.psum_tensor(name, shape, f32))

        def sem(name):
            return ctx.enter_context(nc.semaphore(name))

        idx = sb("idx", [P, QUARTERS * F], i32)
        emb = sb("emb", [P, 2, FD])
        emb_dram = nc.dram_tensor("emb_scratch", (B, FD), f32, kind="Internal").ap()
        rep = sb("rep", [PAIRS, COLS])
        stack = sb("stack", [STACK, COLS], f32r)
        x0t = sb("x0t", [P, TILES_PER_GROUP, J1])
        diag = sb("diag", [P, 2, TB, J1])
        pairs = sb("pairs", [PAIRS, 2, COLS])
        x1 = sb("x1", [P, COLS])
        x1_hi = sb("x1_hi", [P, COLS], f32r)
        x1_lo = sb("x1_lo", [P, COLS], f32r)
        prod = sb("prod", [P, 2, J1, H])
        x2 = sb("x2", [P, 2, H])
        G = sb("G", [P, J1, B])
        w1_hi = sb("w1_hi", [P, F * H], f32r)
        w1_lo = sb("w1_lo", [P, F * H], f32r)
        w2_ring = sb("w2_ring", [P, W2_SLOTS, W2_SLOT * H])
        w_pair = sb("w_pair", [PAIRS, BLOCKS * H])
        sel = sb("sel", [STACK, BLOCKS * PAIRS + J1], f32r)
        mask_low = sb("mask_low", [P, TB + 1])
        mask = mask_low[:, 0:TB]
        low_rows = mask_low[0:STACK, TB:TB + 1]
        z0 = sb("z0", [P, B])
        bias = sb("bias", [P, 2 + M1 + M2])
        bias16 = sb("bias16", [P, 1])
        w3 = sb("w3", [P, M2])
        flat_g = G[:, :, :].rearrange("p j b -> p (j b)")
        w1_raw = flat_g[:, 0:F * H]
        at = F * H
        pair_a_raw = flat_g[0:PAIRS, at:at + BLOCKS * H]
        at += BLOCKS * H
        pair_b_raw = flat_g[0:PAIRS, at:at + BLOCKS * H]
        at += BLOCKS * H
        sel_raw = flat_g[0:STACK, at:at + BLOCKS * PAIRS + J1]
        flat_p = prod[:, :, :, :].rearrange("p a j h -> p (a j h)")
        wt1 = flat_p[:, 0:4 * TOP1].rearrange("p (c n) -> p c n", c=4)
        wt2 = flat_p[:, 4 * TOP1:4 * TOP1 + M1 * TOP2].rearrange("p (c n) -> p c n", c=M1)
        at = 4 * TOP1 + M1 * TOP2
        h1 = flat_p[:, at:at + M1 * B].rearrange("p (c n) -> p c n", c=M1)
        at += M1 * B
        h2 = flat_p[:, at:at + M2 * B].rearrange("p (c n) -> p c n", c=M2)

        at += M2 * B
        z2 = flat_p[:, at:at + B]
        dense = flat_p[0:D, at + B:at + 2 * B]
        y = flat_p[0:1, at + 2 * B:at + 3 * B]

        t_bank = [pb(f"t_bank{i}", [P, COLS]) for i in range(T_BANKS)]
        sel_bank = pb("sel_bank", [P, COLS])
        x1_bank = pb("x1_bank", [P, COLS])
        small_bank = pb("small_bank", [P, COLS])
        g_psum = small_bank[:, 0:TB * J1].rearrange("p (b j) -> p b j", b=TB)
        x0t_psum = t_bank[(CHUNKS - 1) % T_BANKS][:, WIDTH[-1] * H:WIDTH[-1] * H + J1]

        ids_loaded = sem("ids_loaded")
        w_loaded = sem("w_loaded")
        small_loaded = sem("small_loaded")
        ones_set = sem("ones_set")
        bias16_ready = sem("bias16_ready")
        gathered = [sem(f"gathered{q}") for q in range(QUARTERS)]
        emb_stored = [sem(f"emb_stored{q}") for q in range(QUARTERS)]
        w_split_hi = sem("w_split_hi")
        w_split_lo = sem("w_split_lo")
        sel_ready = sem("sel_ready")
        w_pair_ready = sem("w_pair_ready")
        x0_loaded = sem("x0_loaded")
        stack_hi = sem("stack_hi")
        stack_lo = sem("stack_lo")
        x0t_mm = sem("x0t_mm")
        x0t_ready = sem("x0t_ready")
        sel_mm = sem("sel_mm")
        pair_ready = sem("pair_ready")
        pair_mm = sem("pair_mm")
        x1_ready = sem("x1_ready")
        x1_hi_ready = sem("x1_hi_ready")
        x1_lo_ready = sem("x1_lo_ready")
        z0_ready = sem("z0_ready")
        t_mm = sem("t_mm")
        act_scaled = sem("act_scaled")
        dve_scaled = sem("dve_scaled")
        summed = sem("summed")
        folded = sem("folded")
        diag_ready = sem("diag_ready")
        g_mm = sem("g_mm")
        g_copied = sem("g_copied")
        w2_loaded = [sem(f"w2_loaded{i}") for i in range(W2_SLOTS)]
        w2_used = sem("w2_used")
        z2_ready = sem("z2_ready")
        top_loaded = sem("top_loaded")
        top_mm = sem("top_mm")
        h_ready = sem("h_ready")
        y_ready = sem("y_ready")
        y_stored = sem("y_stored")
        block = ctx.enter_context(nc.Block())

        def scaled_before(t, c):
            tile, chunk = (t, c - T_BANKS) if c >= T_BANKS else (t - 1, c - T_BANKS + CHUNKS)
            if chunk in ACT_CHUNKS:
                return act_scaled, tile * NA + (ACT_CHUNKS.index(chunk) + 1)
            return dve_scaled, tile * ND + (DVE_CHUNKS.index(chunk) + 1)

        @block.sync
        def _(sp):
            sp.dma_start(idx[:, :].rearrange("p (q f) -> p q f", q=QUARTERS),
                         ids.rearrange("(q p) f -> p q f", p=P)).then_inc(ids_loaded, 16)
            sp.dma_start(sel_raw, select).then_inc(w_loaded, 16)
            sp.dma_start(pair_a_raw, pair_a).then_inc(w_loaded, 16)
            sp.dma_start(pair_b_raw, pair_b).then_inc(w_loaded, 16)
            sp.dma_start(w1_raw, w1).then_inc(w_loaded, 16)
            for slot in range(2):
                sp.dma_start(prod[:, slot, F, :], b1.to_broadcast([P, H])).then_inc(small_loaded, 16)
            sp.dma_start(mask_low[:, :], consts).then_inc(small_loaded, 16)
            sp.dma_start(bias[:, 0:1], b0).then_inc(small_loaded, 16)
            sp.dma_start(bias[:, 1:2], b2).then_inc(small_loaded, 16)
            sp.dma_start(bias[:, 2:2 + M1], top_b1).then_inc(small_loaded, 16)
            sp.dma_start(bias[:, 2 + M1:], top_b2).then_inc(small_loaded, 16)
            sp.dma_start(w3[:, :], top3).then_inc(small_loaded, 16)
            for i in range(W2_SLOTS):
                sp.dma_start(w2_ring[:, i, :], w2[:, i * W2_SLOT * H:(i + 1) * W2_SLOT * H]).then_inc(w2_loaded[i], 16)

            def load_x0(g):
                src = emb_dram[bass.ds(g * GB, GB), :].rearrange("b (f d) -> f b d", d=D)
                for row in range(0, PAIRS, F):
                    sp.dma_start(rep[row:row + F, :].rearrange("f (b d) -> f b d", d=D), src).then_inc(x0_loaded, 16)

            for q in range(QUARTERS):
                sp.wait_ge(emb_stored[q], 16)
                if q == 0:
                    load_x0(0)
                with sp.Fori(max(q * GROUPS // QUARTERS, 1), (q + 1) * GROUPS // QUARTERS) as g:
                    sp.wait_ge(pair_ready, g * BLOCKS)
                    sp.wait_ge(stack_lo, g)
                    load_x0(g)
            sp.wait_ge(summed, TILES * RED)
            for c in range(3):
                sp.dma_start(wt1[:, c, :], top1[c * P:(c + 1) * P, :]).then_inc(top_loaded, 16)
            sp.dma_start(wt1[0:D, 3, :], top1[3 * P:3 * P + D, :]).then_inc(top_loaded, 16)
            sp.dma_start(dense, dense_t).then_inc(top_loaded, 16)
            sp.dma_start(wt2, top2.rearrange("(c p) n -> p c n", p=P)).then_inc(top_loaded, 16)
            for i in range(W2_SLOTS, W2_LOADS):
                n = min(W2_SLOT, F - i * W2_SLOT)
                sp.wait_ge(w2_used, i - W2_SLOTS + 1)
                sp.dma_start(w2_ring[:, i % W2_SLOTS, 0:n * H],
                             w2[:, i * W2_SLOT * H:(i * W2_SLOT + n) * H]).then_inc(w2_loaded[i % W2_SLOTS], 16)
            sp.wait_ge(y_ready, 1)
            sp.dma_start(out.rearrange("b o -> o b"), y).then_inc(y_stored, 16)
            sp.wait_ge(y_stored, 16)

        @block.gpsimd
        def _(pool):
            pool.memset(x0t[:, :, :], 1.0).then_inc(ones_set, 1)
            pool.wait_ge(ids_loaded, 16)

            def gather(q, f):
                if q >= 2 and f == 0:
                    pool.wait_ge(emb_stored[q - 2], 16)
                pool.indirect_dma_start(
                    out=emb[:, q % 2, f * D:(f + 1) * D], out_offset=None, in_=tables[f],
                    in_offset=bass.IndirectOffsetOnAxis(ap=idx[:, q * F + f:q * F + f + 1], axis=0),
                ).then_inc(gathered[q], 16)

            def store(q):
                pool.wait_ge(gathered[q], 16 * F)
                pool.dma_start(emb_dram[q * P:(q + 1) * P, :], emb[:, q % 2, :]).then_inc(emb_stored[q], 16)

            def diagonal(t, slot, first):
                pool.wait_ge(x0t_ready, t + 1)
                if not first:
                    pool.wait_ge(g_mm, t - 1)
                pool.tensor_tensor(
                    diag[:, slot % 2, :, :],
                    x0t[:, slot:slot + 1, :].to_broadcast([P, TB, J1]),
                    mask.unsqueeze(2).to_broadcast([P, TB, J1]), ALU.mult).then_inc(diag_ready, 1)

            def fold(t, slot):
                ends = 2 * FOLD // UNITS
                pool.wait_ge(act_scaled, t * NA + sum(c < ends for c in ACT_CHUNKS))
                pool.wait_ge(dve_scaled, t * ND + sum(c < ends for c in DVE_CHUNKS))
                pool.tensor_tensor(prod[:, slot % 2, FOLD:2 * FOLD, :], prod[:, slot % 2, FOLD:2 * FOLD, :],
                                   prod[:, slot % 2, 0:FOLD, :], ALU.add).then_inc(folded, 1)

            for f in range(F):
                gather(0, f)
            store(0)
            pool.wait_ge(small_loaded, 16 * SMALL_LOADS)
            left = [(q, f) for q in range(1, QUARTERS) for f in range(F)]

            def gather_some(n):
                for q, f in left[:n]:
                    gather(q, f)
                del left[:n]

            gather_some(AHEAD)

            def group(g, first=False, gathers=False):
                for s in range(TILES_PER_GROUP):
                    t = g * TILES_PER_GROUP + s
                    fold(t, s)
                    diagonal(t, s, first and s < 2)
                    if gathers:
                        gather_some(GATHERS[s])
                        if t % (TILES // QUARTERS) == STORE_AT:
                            store(1 + t // (TILES // QUARTERS))

            for g in range(GROUPS - GROUPS // QUARTERS):
                group(g, first=g == 0, gathers=True)
            with pool.Fori(GROUPS - GROUPS // QUARTERS, GROUPS) as g:
                group(g)

        @block.tensor
        def _(pe):
            def select_pairs(g, b):
                if b == 0:
                    pe.wait_ge(stack_lo, g + 1)
                if not (b == 0 and isinstance(g, int) and g == 0):
                    pe.wait_ge(pair_ready, g * BLOCKS + b)
                pe.matmul(sel_bank[0:ROWS[b], :], sel[:, b * PAIRS:b * PAIRS + ROWS[b]], stack[:, :],
                          start=True, stop=True).then_inc(sel_mm, 1)

            def pair_product(g, b):
                pe.wait_ge(pair_ready, g * BLOCKS + (b + 1))
                if b == 0 and not (isinstance(g, int) and g == 0):
                    pe.wait_ge(x1_ready, g)
                pe.matmul(x1_bank[:, :], w_pair[0:ROWS[b], b * H:(b + 1) * H], pairs[0:ROWS[b], b % 2, :],
                          start=b == 0, stop=b == BLOCKS - 1).then_inc(pair_mm, 1)

            def transpose_x0(s):
                pe.matmul(x0t_psum, stack[:, s * P:(s + 1) * P], sel[:, BLOCKS * PAIRS:],
                          start=True, stop=True).then_inc(x0t_mm, 1)

            def g_product(t, slot):
                pe.wait_ge(summed, (t + 1) * RED)
                pe.wait_ge(diag_ready, t + 1)
                if not (isinstance(t, int) and t == 0):
                    pe.wait_ge(g_copied, t)
                pe.matmul(small_bank[:, 0:TB * J1], x2[:, slot % 2, :],
                          diag[:, slot % 2, :, :].rearrange("p b j -> p (b j)"),
                          start=True, stop=True).then_inc(g_mm, 1)

            def t_chunk(t, s, c, first_tile, last):
                if not (first_tile and c < T_BANKS):
                    pe.wait_ge(*scaled_before(t, c))
                if c == CHUNKS - 1 - T_BANKS:
                    pe.wait_ge(x0t_ready, TILES if last else t + TILES_PER_GROUP)
                if c == CHUNKS - 1 and not last:
                    transpose_x0(s)
                cols = slice(c * COLS, c * COLS + WIDTH[c] * H)
                acc = t_bank[c % T_BANKS][:, 0:WIDTH[c] * H]
                hi, lo = x1_hi[:, s * P:(s + 1) * P], x1_lo[:, s * P:(s + 1) * P]
                pe.matmul(acc, hi, w1_hi[:, cols], start=True, stop=False)
                pe.matmul(acc, hi, w1_lo[:, cols], start=False, stop=False)
                pe.matmul(acc, lo, w1_hi[:, cols], start=False, stop=True).then_inc(t_mm, 1)

            def group(g, first=False, last=False):
                for s in range(TILES_PER_GROUP):
                    t = g * TILES_PER_GROUP + s
                    pe.wait_ge(x1_lo_ready, g * len(PIECES) + (1 if s < 3 else 2))
                    for c in range(CHUNKS):
                        p = s * CHUNKS + c
                        t_chunk(t, s, c, first and s == 0, last)
                        if c == G_AT and not (first and s < 2):
                            g_product(t - 2, s)
                        if not last:
                            if p in SEL_AT:
                                select_pairs(g + 1, SEL_AT.index(p))
                            if p in PAIR_AT:
                                pair_product(g + 1, PAIR_AT.index(p))

            pe.wait_ge(sel_ready, 1)
            pe.wait_ge(w_pair_ready, 1)
            for b in range(BLOCKS):
                select_pairs(0, b)
                if b < TILES_PER_GROUP:
                    if b > 0:
                        pe.wait_ge(x0t_ready, b)
                    transpose_x0(b)
                if b > 0:
                    pair_product(0, b - 1)
            pair_product(0, BLOCKS - 1)
            pe.wait_ge(w_split_lo, 1)
            group(0, first=True)
            with pe.Fori(1, GROUPS - 1) as g:
                group(g)
            group(GROUPS - 1, last=True)
            g_product(TILES - 2, 0)
            g_product(TILES - 1, 1)

            pe.wait_ge(g_copied, TILES)
            for j in range(F):
                i, k = j // W2_SLOT, j % W2_SLOT
                if k == 0:
                    pe.wait_ge(w2_loaded[i % W2_SLOTS], 16 * (i // W2_SLOTS + 1))
                mm = pe.matmul(t_bank[0][:, :], w2_ring[:, i % W2_SLOTS, k * H:(k + 1) * H], G[:, j, :],
                               start=j == 0, stop=j == F - 1)
                if k == W2_SLOT - 1 or j == F - 1:
                    mm.then_inc(w2_used, 1)

            pe.wait_ge(top_loaded, 16 * TOP_LOADS)
            pe.wait_ge(z0_ready, GROUPS)
            feats = [z0[:, :], G[:, F, :], dense, z2]
            weights = [(0, P), (1, P), (3, D), (2, P)]
            for m in range(M1):
                for n in range(3):
                    w, k = weights[n]
                    pe.matmul(t_bank[1 + m][:, :], wt1[0:k, w, m * P:(m + 1) * P], feats[n],
                              start=n == 0, stop=False)
            pe.wait_ge(z2_ready, 1)
            for m in range(M1):
                pe.matmul(t_bank[1 + m][:, :], wt1[:, 2, m * P:(m + 1) * P], feats[3],
                          start=False, stop=True).then_inc(top_mm, 1)
            for m in range(M2):
                for c in range(M1):
                    pe.wait_ge(h_ready, c + 1)
                    mm = pe.matmul((sel_bank, x1_bank)[m][:, :], wt2[:, c, m * P:(m + 1) * P], h1[:, c, :],
                                   start=c == 0, stop=c == M1 - 1)
                mm.then_inc(top_mm, 1)
            for m in range(M2):
                pe.wait_ge(h_ready, M1 + m + 1)
                mm = pe.matmul(small_bank[0:1, :], w3[:, m:m + 1], h2[:, m, :], start=m == 0, stop=m == M2 - 1)
            mm.then_inc(top_mm, 1)

        @block.scalar
        def _(act):
            def copy_x0t(g, s, first):
                t = g * TILES_PER_GROUP + s
                act.wait_ge(x0t_mm, t + 1)
                if not first:
                    prev = t - TILES_PER_GROUP
                    act.wait_ge(act_scaled, (prev + 1) * NA)
                    act.wait_ge(dve_scaled, (prev + 1) * ND)
                    act.wait_ge(diag_ready, prev + 1)
                act.activation(x0t[:, s, 0:F], x0t_psum[:, 0:F], ACT.Copy).then_inc(x0t_ready, 1)

            def split_x0_hi(g, first):
                act.wait_ge(x0_loaded, (g + 1) * (16 * X0_COPIES))
                if not first:
                    act.wait_ge(x0t_mm, g * TILES_PER_GROUP)
                    act.wait_ge(sel_mm, g * BLOCKS)
                act.activation(stack[:, :], rep[0:STACK, :], ACT.Copy).then_inc(stack_hi, 1)

            def bias_x1(g, first):
                act.wait_ge(pair_mm, (g + 1) * BLOCKS)
                if not first:
                    act.wait_ge(x1_lo_ready, g * len(PIECES))
                    act.wait_ge(z0_ready, g)
                act.activation(x1[:, :], x1_bank[:, :], ACT.Identity, bias=bias[:, 0:1]).then_inc(x1_ready, 1)

            def split_x1_hi(g, i, first):
                a, b = PIECES[i]
                act.wait_ge(x1_ready, g + 1)
                if not first:
                    act.wait_ge(t_mm, (g - 1) * (TILES_PER_GROUP * CHUNKS) + b * CHUNKS)
                act.activation(x1_hi[:, a * P:b * P], x1[:, a * P:b * P], ACT.Copy).then_inc(x1_hi_ready, 1)

            def copy_g(t, g, s):
                act.wait_ge(g_mm, t + 1)
                act.activation(G[:, :, bass.ds(g * GB + s * TB, TB)].rearrange("p j b -> p b j"),
                               g_psum, ACT.Copy).then_inc(g_copied, 1)

            def scale_chunk(t, s, c, first):
                act.wait_ge(t_mm, t * CHUNKS + (c + 1))
                if c == ACT_CHUNKS[0]:
                    act.wait_ge(x0t_ready, t + 1)
                    if not (first and s < 2):
                        act.wait_ge(summed, (t - 1) * RED)
                for u in range(WIDTH[c]):
                    j = c * UNITS + u
                    last = act.activation(prod[:, s % 2, j, :], t_bank[c % T_BANKS][:, u * H:(u + 1) * H],
                                          ACT.Copy, scale=x0t[:, s, j:j + 1])
                last.then_inc(act_scaled, 1)

            def group(g, first=False, last=False):
                for s in range(TILES_PER_GROUP):
                    t = g * TILES_PER_GROUP + s
                    for c in ACT_CHUNKS:
                        scale_chunk(t, s, c, first)
                        if s == 0 and c == 1:
                            split_x1_hi(g, 1, first)
                        if c == 0:
                            if s > 0 and not last:
                                copy_x0t(g + 1, s - 1, False)
                            if s == 0 and not first:
                                copy_x0t(g, TILES_PER_GROUP - 1, False)
                        if c == G_COPY_AT and not (first and s < 2):
                            copy_g(t - 2, g if s >= 2 else g - 1, (s - 2) % TILES_PER_GROUP)
                        if not last:
                            if s == 0 and c == 1:
                                split_x0_hi(g + 1, False)
                            if s == 3 and c == BIAS_AT:
                                bias_x1(g + 1, False)
                                split_x1_hi(g + 1, 0, False)

            act.wait_ge(w_loaded, 16 * 4)
            act.activation(sel[:, :], sel_raw, ACT.Copy).then_inc(sel_ready, 1)
            act.activation(w1_hi[:, :], w1_raw, ACT.Copy).then_inc(w_split_hi, 1)
            act.wait_ge(ones_set, 1)
            act.wait_ge(small_loaded, 16 * SMALL_LOADS)
            split_x0_hi(0, True)
            for s in range(TILES_PER_GROUP):
                copy_x0t(0, s, True)
            bias_x1(0, True)
            split_x1_hi(0, 0, True)
            group(0, first=True)
            with act.Fori(1, GROUPS - 1) as g:
                group(g)
            group(GROUPS - 1, last=True)
            copy_g(TILES - 2, GROUPS - 1, 2)
            copy_g(TILES - 1, GROUPS - 1, 3)
            act.wait_ge(bias16_ready, 1)
            act.wait_ge(w2_used, W2_LOADS)
            act.activation(z2, t_bank[0][:, :], ACT.Identity, bias=bias16[:, 0:1]).then_inc(z2_ready, 1)
            for m in range(M1):
                act.wait_ge(top_mm, m + 1)
                act.activation(h1[:, m, :], t_bank[1 + m][:, :], ACT.Relu, bias=bias[:, 2 + m:3 + m]).then_inc(h_ready, 1)
            for m in range(M2):
                act.wait_ge(top_mm, M1 + m + 1)
                act.activation(h2[:, m, :], (sel_bank, x1_bank)[m][:, :], ACT.Relu,
                               bias=bias[:, 2 + M1 + m:3 + M1 + m]).then_inc(h_ready, 1)
            act.wait_ge(top_mm, M1 + M2 + 1)
            act.activation(y, small_bank[0:1, :], ACT.Copy).then_inc(y_ready, 1)

        @block.vector
        def _(dve):
            def split_x0_lo(g):
                dve.wait_ge(stack_hi, g + 1)
                dve.scalar_tensor_tensor(out=stack[:, :], in0=rep[0:STACK, :], scalar=low_rows, in1=stack[:, :],
                                         op0=ALU.mult, op1=ALU.subtract).then_inc(stack_lo, 1)

            def form_pairs(g, b, first):
                dve.wait_ge(sel_mm, g * BLOCKS + (b + 1))
                if not (first and b < 2):
                    dve.wait_ge(pair_mm, g * BLOCKS + max(b - 1, 0))
                dve.tensor_tensor(pairs[0:ROWS[b], b % 2, :], sel_bank[0:ROWS[b], :], rep[0:ROWS[b], :],
                                  ALU.mult).then_inc(pair_ready, 1)

            def split_x1_lo(g, i):
                a, b = PIECES[i]
                dve.wait_ge(x1_hi_ready, g * len(PIECES) + (i + 1))
                dve.tensor_tensor(x1_lo[:, a * P:b * P], x1[:, a * P:b * P], x1_hi[:, a * P:b * P],
                                  ALU.subtract).then_inc(x1_lo_ready, 1)

            def sum_z0(g):
                dve.wait_ge(x1_ready, g + 1)
                dve.tensor_reduce(z0[:, bass.ds(g * GB, GB)],
                                  x1[:, :].rearrange("p (b d) -> p b d", d=D), AX.X, ALU.add)\
                   .then_inc(z0_ready, 1)

            def scale_chunk(t, s, c, first):
                dve.wait_ge(t_mm, t * CHUNKS + (c + 1))
                if c == DVE_CHUNKS[0]:
                    dve.wait_ge(x0t_ready, t + 1)
                    if not (first and s < 2):
                        dve.wait_ge(summed, (t - 1) * RED)
                j, n = c * UNITS, WIDTH[c]
                dve.tensor_tensor(prod[:, s % 2, j:j + n, :],
                                  t_bank[c % T_BANKS][:, 0:n * H].rearrange("p (j h) -> p j h", h=H),
                                  x0t[:, s, j:j + n].unsqueeze(2).to_broadcast([P, n, H]),
                                  ALU.mult).then_inc(dve_scaled, 1)

            def sum_over_j(t, slot, i, first):
                if i == 0:
                    dve.wait_ge(act_scaled, (t + 1) * NA)
                    dve.wait_ge(dve_scaled, (t + 1) * ND)
                    dve.wait_ge(folded, t + 1)
                    if not first:
                        dve.wait_ge(g_mm, t - 1)
                h = slice(i * HR, (i + 1) * HR)
                dve.tensor_reduce(x2[:, slot % 2, h], prod[:, slot % 2, FOLD:, h].rearrange("p j h -> p h j"),
                                  AX.X, ALU.add).then_inc(summed, 1)

            def group(g, first=False, last=False):
                for s in range(TILES_PER_GROUP):
                    t = g * TILES_PER_GROUP + s
                    for c in range(CHUNKS):
                        p = s * CHUNKS + c
                        if c in DVE_CHUNKS:
                            scale_chunk(t, s, c, first)
                        if not last:
                            if p in SEL_AT:
                                form_pairs(g + 1, SEL_AT.index(p), False)
                            if p == 2:
                                split_x0_lo(g + 1)
                            if p == X1_LO_AT:
                                split_x1_lo(g + 1, 0)
                            if p == Z0_AT:
                                sum_z0(g + 1)
                        if p == 2:
                            split_x1_lo(g, 1)
                        if c in SUM_AT and not (first and s == 0):
                            sum_over_j(t - 1, s + 1, SUM_AT.index(c), first and s < 3)

            dve.wait_ge(w_loaded, 16 * 4)
            dve.tensor_tensor(w_pair[:, :], pair_a_raw, pair_b_raw, ALU.add).then_inc(w_pair_ready, 1)
            dve.wait_ge(w_split_hi, 1)
            dve.tensor_tensor(w1_lo[:, :], w1_raw, w1_hi[:, :], ALU.subtract).then_inc(w_split_lo, 1)
            dve.wait_ge(small_loaded, 16 * SMALL_LOADS)
            dve.tensor_scalar(bias16[:, :], bias[:, 1:2], float(D), None, ALU.mult).then_inc(bias16_ready, 1)
            split_x0_lo(0)
            for b in range(BLOCKS):
                form_pairs(0, b, True)
            split_x1_lo(0, 0)
            sum_z0(0)
            group(0, first=True)
            with dve.Fori(1, GROUPS - 1) as g:
                group(g)
            group(GROUPS - 1, last=True)
            for i in range(RED):
                sum_over_j(TILES - 1, 1, i, False)


def kernel(**inputs):
    import numpy as np
    import concourse.bacc as _bacc
    from concourse.bass_utils import run_bass_kernel_spmd as _run

    w0 = np.asarray(inputs["L0_rec_W0"]).reshape(H, F, F)
    zero = np.zeros((F, H), w0.dtype)

    def shifted(w, first):
        wide = np.concatenate([w, w], axis=1).reshape(F * 2 * F, H)
        rows = [wide[s:s + (F - 1) * (2 * F + 1) + 1:2 * F + 1] for s in range(SHIFTS)]
        if not first:
            rows[0] = zero
        rows += [zero] * (BLOCKS * PER_BLOCK - SHIFTS)
        return np.ascontiguousarray(np.stack(rows).reshape(BLOCKS, PAIRS, H).transpose(1, 0, 2)).reshape(PAIRS, BLOCKS * H)

    def by_k(w):
        return np.ascontiguousarray(np.asarray(w).reshape(H, F, H).transpose(2, 1, 0)).reshape(H, F * H)

    select = np.zeros((STACK, BLOCKS * PAIRS + J1), np.float32)
    for row, sign in ((0, -1.0), (F, 1.0)):
        for s in range(SHIFTS):
            for j in range(F):
                select[row + (j + s) % F, s * F + j] = sign
        for j in range(F):
            select[row + j, BLOCKS * PAIRS + j] = sign
    masks = np.zeros((P, TB + 1), np.float32)
    for p in range(P):
        masks[p, p // D] = 1.0
        masks[p, TB] = float(p >= F)

    arrays = {
        "ids": np.ascontiguousarray(inputs["ids"]),
        "dense_t": np.ascontiguousarray(np.asarray(inputs["dense_ctx"]).T),
        "pair_a": shifted(w0.transpose(1, 2, 0), True),
        "pair_b": shifted(w0.transpose(2, 1, 0), False),
        "w1": by_k(inputs["L0_rec_W1"]),
        "w2": by_k(inputs["L0_rec_W2"]),
        "b0": np.asarray(inputs["L0_rec_b0"]).reshape(H, 1),
        "b1": np.asarray(inputs["L0_rec_b1"]).reshape(1, H),
        "b2": np.asarray(inputs["L0_rec_b2"]).reshape(H, 1),
        "top1": np.ascontiguousarray(inputs["W_top1"]),
        "top_b1": np.ascontiguousarray(np.asarray(inputs["b_top1"]).reshape(M1, P).T),
        "top2": np.ascontiguousarray(inputs["W_top2"]),
        "top_b2": np.ascontiguousarray(np.asarray(inputs["b_top2"]).reshape(M2, P).T),
        "top3": np.ascontiguousarray(np.asarray(inputs["W_top3"]).reshape(M2, P).T),
        "select": select,
        "consts": masks,
    }
    for f in range(F):
        arrays[f"tbl_{f}"] = np.ascontiguousarray(inputs[f"tbl_{f}"])

    nc = _bacc.Bacc("TRN2", target_bir_lowering=False, num_devices=1)
    aps = {n: nc.dram_tensor(f"in_{n}", a.shape, mybir.dt.from_np(a.dtype), kind="ExternalInput").ap()
           for n, a in arrays.items()}
    out = nc.dram_tensor("out_y", (B, 1), mybir.dt.float32, kind="ExternalOutput").ap()
    tables = [aps.pop(f"tbl_{f}") for f in range(F)]
    tower_program(nc, tables=tables, out=out, **aps)
    r = _run(nc, [{f"in_{n}": a for n, a in arrays.items()}], core_ids=[0])
    return r.results[0]["out_y"]
```

```python
from contextlib import ExitStack

import concourse.bass as bass
from concourse import mybir

B, F, D, H = 512, 39, 16, 128
P = 128
COLS = 512
TILES_PER_GROUP = COLS // P
GROUPS = B * D // COLS
TILES = GROUPS * TILES_PER_GROUP
GB = COLS // D
TB = P // D
GROUP_ROWS = GB * F
GATHERS = -(-GROUP_ROWS // P)
ROW_PARTS = -(-GROUP_ROWS // GATHERS)
SLOT_ROWS = ROW_PARTS * GATHERS
J1 = F + 1
COPIES = P // F
PAIRS = COPIES * F
BLOCKS = -(-(F // 2 + 1) // COPIES)
REP_ROWS = PAIRS + BLOCKS - 1
UNITS = COLS // H
CHUNKS = -(-F // UNITS)
WIDTH = [min(UNITS, F - UNITS * c) for c in range(CHUNKS)]
T_BANKS = 5
ACT_CHUNKS = [0, 1, 3, 5, 7, 9]
DVE_CHUNKS = [c for c in range(CHUNKS) if c not in ACT_CHUNKS]
NA, ND = len(ACT_CHUNKS), len(DVE_CHUNKS)
SECOND_SLOTS = 3
SLOT_USES = (BLOCKS - 1) // SECOND_SLOTS
RED = 4
HR = H // RED
X0_LOADS = COPIES + 1
W2_SLOT = 3
W2_LOADS = -(-F // W2_SLOT)
W2_SLOTS = 3
SPLIT_W2_SLOTS = 6
SPLIT_G_SLOTS = 4
SMALL_LOADS = 9
WARM_UP = (5, 3, 0, 2)
WT1_LOADS = 3
PIECES = [(0, 3), (3, 4)]
FOLD = 10
TOP1, TOP2 = 512, 256
M1, M2 = TOP1 // P, TOP2 // P
FORM_AT = [6 + 4 * b for b in range(BLOCKS)]
PAIR_AT = [p + 5 for p in FORM_AT]
X0T_AT = 8
AHEAD = 2
GATHERS_EARLY = 4
GATHERS_AT = (4, 2, 0, 0)
G_AT = 5
G_COPY_AT = 7
BIAS_AT = 5
X1_LO_AT = 36
X1_LO_LAST_AT = 2
HALVINGS = 3
Z0_TILE = 1
SUM_AT = (1, 3, 5, 7)


def tower_program(nc, ids, starts, table, dense_t, pair_a, pair_b, w1, w2, b0, b1, b2,
                  top1, top_b1, top2, top_b2, top3, identity, sample_mask, out):
    f32, f32r, i32 = mybir.dt.float32, mybir.dt.float32r, mybir.dt.int32
    ALU = mybir.AluOpType
    ACT = mybir.ActivationFunctionType
    AX = mybir.AxisListType
    ctx = ExitStack()
    with ctx:
        def sb(name, shape, dt=f32):
            return ctx.enter_context(nc.sbuf_tensor(name, shape, dt))

        def pb(name, shape):
            return ctx.enter_context(nc.psum_tensor(name, shape, f32))

        def sem(name):
            return ctx.enter_context(nc.semaphore(name))

        ids_all = sb("ids_all", [ROW_PARTS, GROUPS * GATHERS], i32)
        table_at = sb("table_at", [ROW_PARTS, GATHERS], i32)
        idx = sb("idx", [ROW_PARTS, GATHERS], i32)
        emb = sb("emb", [ROW_PARTS, GATHERS * D])
        emb_dram = nc.dram_tensor("emb_scratch", (GROUPS * ROW_PARTS, GATHERS * D), f32, kind="Internal").ap()
        rep = sb("rep", [REP_ROWS, COLS])
        first = sb("first", [PAIRS, COLS])
        second = sb("second", [PAIRS, SECOND_SLOTS, COLS])
        x0t = sb("x0t", [P, TILES_PER_GROUP, J1])
        diag = sb("diag", [P, 2, TB, J1])
        pairs = sb("pairs", [PAIRS, 2, COLS])
        x1 = sb("x1", [P, COLS])
        x1_hi = sb("x1_hi", [P, COLS], f32r)
        x1_lo = sb("x1_lo", [P, COLS], f32r)
        prod = sb("prod", [P, 2, J1, H])
        x2 = sb("x2", [P, 2, H])
        G = sb("G", [P, J1, B])
        w1_hi = sb("w1_hi", [P, F * H], f32r)
        w1_lo = sb("w1_lo", [P, F * H], f32r)
        w2_ring = sb("w2_ring", [P, W2_SLOTS, W2_SLOT * H])
        w_pair = sb("w_pair", [PAIRS, BLOCKS * H])
        ident = sb("ident", [F, F])
        mask = sb("mask", [P, TB])
        z0 = sb("z0", [P, B])
        bias = sb("bias", [P, 2 + M1 + M2])
        bias16 = sb("bias16", [P, 1])
        wt1 = sb("wt1", [P, 4, TOP1])
        dense = sb("dense", [D, B])
        w3 = sb("w3", [P, M2])
        flat_g = G[:, :, :].rearrange("p j b -> p (j b)")
        w1_raw = flat_g[:, 0:F * H]
        at = F * H
        pair_a_raw = flat_g[0:PAIRS, at:at + BLOCKS * H]
        at += BLOCKS * H
        pair_b_raw = flat_g[0:PAIRS, at:at + BLOCKS * H]
        g_hi = w1_hi[:, 0:SPLIT_G_SLOTS * B].rearrange("p (s b) -> p s b", b=B)
        g_lo = w1_hi[:, SPLIT_G_SLOTS * B:2 * SPLIT_G_SLOTS * B].rearrange("p (s b) -> p s b", b=B)
        at = SPLIT_W2_SLOTS * W2_SLOT * H
        w2_hi = w1_lo[:, 0:at].rearrange("p (s n) -> p s n", s=SPLIT_W2_SLOTS)
        w2_lo = w1_lo[:, at:2 * at].rearrange("p (s n) -> p s n", s=SPLIT_W2_SLOTS)
        flat_p = prod[:, :, :, :].rearrange("p a j h -> p (a j h)")
        wt2 = flat_p[:, 0:M1 * TOP2].rearrange("p (c n) -> p c n", c=M1)
        at = M1 * TOP2
        h1 = flat_p[:, at:at + M1 * B].rearrange("p (c n) -> p c n", c=M1)
        at += M1 * B
        h2 = flat_p[:, at:at + M2 * B].rearrange("p (c n) -> p c n", c=M2)
        at += M2 * B
        z2 = flat_p[:, at:at + B]
        y = flat_p[0:1, at + B:at + 2 * B]

        t_bank = [pb(f"t_bank{i}", [P, COLS]) for i in range(T_BANKS)]
        x0t_bank = pb("x0t_bank", [P, COLS])
        x1_bank = pb("x1_bank", [P, COLS])
        small_bank = pb("small_bank", [P, COLS])
        h1_bank = [x1_bank, x0t_bank, t_bank[2], t_bank[3]]
        h2_bank = [t_bank[1], t_bank[4]]
        g_psum = small_bank[:, 0:TB * J1].rearrange("p (b j) -> p b j", b=TB)
        x0t_psum = x0t_bank[:, 0:TILES_PER_GROUP * F].rearrange("p (s f) -> p s f", f=F)

        ids_loaded = sem("ids_loaded")
        w_loaded = sem("w_loaded")
        small_loaded = sem("small_loaded")
        ones_set = sem("ones_set")
        bias16_ready = sem("bias16_ready")
        index_ready = sem("index_ready")
        gathered = sem("gathered")
        emb_stored = sem("emb_stored")
        w_split_hi = sem("w_split_hi")
        w_split_lo = sem("w_split_lo")
        w_pair_ready = sem("w_pair_ready")
        x0_loaded = sem("x0_loaded")
        first_ready = sem("first_ready")
        second_ready = [sem(f"second_ready{i}") for i in range(SECOND_SLOTS)]
        x0t_mm = sem("x0t_mm")
        x0t_ready = sem("x0t_ready")
        pair_ready = sem("pair_ready")
        pair_mm = sem("pair_mm")
        x1_ready = sem("x1_ready")
        x1_hi_ready = sem("x1_hi_ready")
        x1_lo_ready = sem("x1_lo_ready")
        halved = sem("halved")
        z0_ready = sem("z0_ready")
        t_mm = sem("t_mm")
        act_scaled = sem("act_scaled")
        dve_scaled = sem("dve_scaled")
        summed = sem("summed")
        folded = sem("folded")
        diag_ready = sem("diag_ready")
        g_mm = sem("g_mm")
        g_copied = sem("g_copied")
        w2_loaded = [sem(f"w2_loaded{i}") for i in range(W2_SLOTS)]
        w2_hi_ready = sem("w2_hi_ready")
        w2_lo_ready = sem("w2_lo_ready")
        g_hi_ready = sem("g_hi_ready")
        g_lo_ready = sem("g_lo_ready")
        z2_mm = sem("z2_mm")
        z2_ready = sem("z2_ready")
        wt1_loaded = sem("wt1_loaded")
        wt2_loaded = sem("wt2_loaded")
        top_mm = sem("top_mm")
        h_ready = sem("h_ready")
        y_ready = sem("y_ready")
        y_stored = sem("y_stored")
        block = ctx.enter_context(nc.Block())

        def scaled_before(t, c):
            tile, chunk = (t, c - T_BANKS) if c >= T_BANKS else (t - 1, c - T_BANKS + CHUNKS)
            if chunk in ACT_CHUNKS:
                return act_scaled, tile * NA + (ACT_CHUNKS.index(chunk) + 1)
            return dve_scaled, tile * ND + (DVE_CHUNKS.index(chunk) + 1)

        @block.sync
        def _(sp):
            sp.dma_start(ids_all[:, :], ids).then_inc(ids_loaded, 16)
            sp.dma_start(table_at[:, :], starts).then_inc(ids_loaded, 16)
            sp.dma_start(pair_a_raw, pair_a).then_inc(w_loaded, 16)
            sp.dma_start(pair_b_raw, pair_b).then_inc(w_loaded, 16)
            sp.dma_start(w1_raw, w1).then_inc(w_loaded, 16)
            for slot in range(2):
                sp.dma_start(prod[:, slot, F, :], b1.to_broadcast([P, H])).then_inc(small_loaded, 16)
            sp.dma_start(mask[:, :], sample_mask).then_inc(small_loaded, 16)
            sp.dma_start(ident[:, :], identity).then_inc(small_loaded, 16)
            sp.dma_start(bias[:, 0:1], b0).then_inc(small_loaded, 16)
            sp.dma_start(bias[:, 1:2], b2).then_inc(small_loaded, 16)
            sp.dma_start(bias[:, 2:2 + M1], top_b1).then_inc(small_loaded, 16)
            sp.dma_start(bias[:, 2 + M1:], top_b2).then_inc(small_loaded, 16)
            sp.dma_start(w3[:, :], top3).then_inc(small_loaded, 16)

            emb_rows = emb_dram.rearrange("p (i d) -> (p i) d", d=D)

            def store_rows(g):
                sp.wait_ge(gathered, (g + 1) * (16 * GATHERS))
                sp.dma_start(emb_dram[bass.ds(g * ROW_PARTS, ROW_PARTS), :], emb[:, :]).then_inc(emb_stored, 16)

            def load_x0(g, at_once):
                sp.wait_ge(emb_stored, (g + 1) * 16)
                src = emb_rows[bass.ds(g * SLOT_ROWS, GROUP_ROWS), :].rearrange("(b f) d -> f b d", f=F)
                for row in range(0, REP_ROWS, F):
                    n = min(F, REP_ROWS - row)
                    if row == 0 or at_once:
                        sp.dma_start(rep[row:row + n, :].rearrange("f (b d) -> f b d", d=D), src[0:n]).then_inc(x0_loaded, 16)
                    else:
                        if row == F:
                            sp.wait_ge(x0_loaded, g * (16 * X0_LOADS) + 16)
                        sp.dma_start(rep[row:row + n, :], rep[0:n, :]).then_inc(x0_loaded, 16)

            def factors(g):
                sp.wait_ge(x0_loaded, (g + 1) * (16 * X0_LOADS))
                for i in range(COPIES):
                    row = -i * BLOCKS % F
                    sp.dma_start(first[i * F:(i + 1) * F, :], rep[row:row + F, :]).then_inc(first_ready, 16)
                for b in range(1, BLOCKS):
                    if b > SECOND_SLOTS:
                        sp.wait_ge(pair_ready, g * BLOCKS + (b + 1 - SECOND_SLOTS))
                    k = (b - 1) % SECOND_SLOTS
                    sp.dma_start(second[:, k, :], rep[b:b + PAIRS, :]).then_inc(second_ready[k], 16)

            store_rows(0)
            load_x0(0, at_once=True)
            factors(0)
            for i in range(W2_SLOTS):
                sp.dma_start(w2_ring[:, i, :], w2[:, i * W2_SLOT * H:(i + 1) * W2_SLOT * H]).then_inc(w2_loaded[i], 16)
            sp.dma_start(wt1[:, 0:3, :], top1[0:3 * P, :].rearrange("(c p) n -> p c n", p=P)).then_inc(wt1_loaded, 16)
            sp.dma_start(wt1[0:D, 3, :], top1[3 * P:, :]).then_inc(wt1_loaded, 16)
            sp.dma_start(dense[:, :], dense_t).then_inc(wt1_loaded, 16)

            def next_group(g, at_once):
                sp.wait_ge(pair_ready, g * BLOCKS)
                sp.wait_ge(x0t_mm, g)
                store_rows(g)
                load_x0(g, at_once)
                factors(g)

            next_group(1, at_once=True)
            with sp.Fori(2, GROUPS) as g:
                next_group(g, at_once=False)
            for i in range(W2_SLOTS, W2_LOADS):
                n = min(W2_SLOT, F - i * W2_SLOT)
                sp.wait_ge(w2_lo_ready, i - W2_SLOTS + 1)
                sp.dma_start(w2_ring[:, i % W2_SLOTS, 0:n * H],
                             w2[:, i * W2_SLOT * H:(i * W2_SLOT + n) * H]).then_inc(w2_loaded[i % W2_SLOTS], 16)
            sp.wait_ge(summed, TILES * RED)
            sp.dma_start(wt2, top2.rearrange("(c p) n -> p c n", p=P)).then_inc(wt2_loaded, 16)
            sp.wait_ge(y_ready, 1)
            sp.dma_start(out.rearrange("b o -> o b"), y).then_inc(y_stored, 16)
            sp.wait_ge(y_stored, 16)

        @block.gpsimd
        def _(pool):
            pool.memset(x0t[:, :, :], 1.0).then_inc(ones_set, 1)
            pool.wait_ge(ids_loaded, 16 * 2)

            def index(g, first=False):
                if not first:
                    pool.wait_ge(gathered, g * (16 * GATHERS))
                pool.tensor_tensor(idx[:, :], ids_all[:, bass.ds(g * GATHERS, GATHERS)], table_at[:, :],
                                   ALU.add).then_inc(index_ready, 1)
                pool.wait_ge(index_ready, g + 1)
                if not first:
                    pool.wait_ge(emb_stored, g * 16)

            def gather(i):
                pool.indirect_dma_start(
                    out=emb[:, i * D:(i + 1) * D], out_offset=None, in_=table,
                    in_offset=bass.IndirectOffsetOnAxis(ap=idx[:, i:i + 1], axis=0),
                ).then_inc(gathered, 16)

            def diagonal(t, slot, first):
                pool.wait_ge(x0t_ready, t + 1)
                if not first:
                    pool.wait_ge(g_mm, t - 1)
                pool.tensor_tensor(
                    diag[:, slot % 2, :, :],
                    x0t[:, slot:slot + 1, :].to_broadcast([P, TB, J1]),
                    mask[:, :].unsqueeze(2).to_broadcast([P, TB, J1]), ALU.mult).then_inc(diag_ready, 1)

            def fold(t, slot):
                ends = -(-2 * FOLD // UNITS)
                pool.wait_ge(act_scaled, t * NA + sum(c < ends for c in ACT_CHUNKS))
                pool.wait_ge(dve_scaled, t * ND + sum(c < ends for c in DVE_CHUNKS))
                pool.tensor_tensor(prod[:, slot % 2, FOLD:2 * FOLD, :], prod[:, slot % 2, FOLD:2 * FOLD, :],
                                   prod[:, slot % 2, 0:FOLD, :], ALU.add).then_inc(folded, 1)

            def sum_z0(g):
                pool.wait_ge(x1_lo_ready, (g + 1) * len(PIECES))
                by_d = x1[:, :].rearrange("p (b d) -> p b d", d=D)
                n, halvings = D // 2, 0
                while n > 1:
                    pool.tensor_tensor(by_d[:, :, 0:n], by_d[:, :, 0:n], by_d[:, :, n:2 * n], ALU.add).then_inc(halved, 1)
                    n, halvings = n // 2, halvings + 1
                    pool.wait_ge(halved, g * HALVINGS + halvings)
                pool.tensor_tensor(z0[:, bass.ds(g * GB, GB)].unsqueeze(2), by_d[:, :, 0:1], by_d[:, :, 1:2],
                                   ALU.add).then_inc(z0_ready, 1)

            for g in range(AHEAD):
                index(g, first=g == 0)
                for i in range(GATHERS):
                    gather(i)
            pool.wait_ge(small_loaded, 16 * SMALL_LOADS)

            index(AHEAD)
            for i in range(GATHERS_EARLY):
                gather(i)

            def group(g, first=False, gathers=True, early=True):
                for s in range(TILES_PER_GROUP):
                    t = g * TILES_PER_GROUP + s
                    fold(t, s)
                    if early and s == TILES_PER_GROUP - 1:
                        index(g + AHEAD + 1)
                    diagonal(t, s, first and s < 2)
                    if s == Z0_TILE:
                        sum_z0(g)
                    if gathers:
                        begin = GATHERS_EARLY + sum(GATHERS_AT[:s])
                        for i in range(begin, begin + GATHERS_AT[s]):
                            gather(i)
                if early:
                    for i in range(GATHERS_EARLY):
                        gather(i)

            group(0, first=True)
            with pool.Fori(1, GROUPS - AHEAD - 1) as g:
                group(g)
            group(GROUPS - AHEAD - 1, early=False)
            with pool.Fori(GROUPS - AHEAD, GROUPS) as g:
                group(g, gathers=False, early=False)
            pool.wait_ge(t_mm, TILES * CHUNKS)
            for i in range(W2_LOADS):
                slot, n = i % SPLIT_W2_SLOTS, min(W2_SLOT, F - i * W2_SLOT) * H
                raw = w2_ring[:, i % W2_SLOTS, 0:n]
                pool.wait_ge(w2_loaded[i % W2_SLOTS], 16 * (i // W2_SLOTS + 1))
                if i >= SPLIT_W2_SLOTS:
                    pool.wait_ge(z2_mm, (i - SPLIT_W2_SLOTS + 1) * W2_SLOT)
                if i >= W2_SLOTS:
                    pool.tensor_copy(w2_hi[:, slot, 0:n], raw).then_inc(w2_hi_ready, 1)
                pool.wait_ge(w2_hi_ready, i + 1)
                pool.tensor_tensor(w2_lo[:, slot, 0:n], raw, w2_hi[:, slot, 0:n],
                                   ALU.subtract).then_inc(w2_lo_ready, 1)

        @block.tensor
        def _(pe):
            def pair_product(g, b):
                pe.wait_ge(pair_ready, g * BLOCKS + (b + 1))
                if b == 0 and not (isinstance(g, int) and g == 0):
                    pe.wait_ge(x1_ready, g)
                pe.matmul(x1_bank[:, :], w_pair[:, b * H:(b + 1) * H], pairs[:, b % 2, :],
                          start=b == 0, stop=b == BLOCKS - 1).then_inc(pair_mm, 1)

            def transpose_x0(g, first):
                if first:
                    pe.wait_ge(x0_loaded, 16 * X0_LOADS)
                for s in range(TILES_PER_GROUP):
                    mm = pe.transpose(x0t_psum[:, s, :], rep[0:F, s * P:(s + 1) * P], ident[:, :])
                mm.then_inc(x0t_mm, 1)

            def g_product(t, slot):
                pe.wait_ge(summed, (t + 1) * RED)
                pe.wait_ge(diag_ready, t + 1)
                if not (isinstance(t, int) and t == 0):
                    pe.wait_ge(g_copied, t)
                pe.matmul(small_bank[:, 0:TB * J1], x2[:, slot % 2, :],
                          diag[:, slot % 2, :, :].rearrange("p b j -> p (b j)"),
                          start=True, stop=True).then_inc(g_mm, 1)

            def t_chunk(t, s, c, first_tile, then_x0t):
                if then_x0t is not None:
                    pe.wait_ge(x0_loaded, (then_x0t + 1) * (16 * X0_LOADS))
                    pe.wait_ge(x0t_ready, then_x0t * TILES_PER_GROUP)
                if not (first_tile and c < T_BANKS):
                    pe.wait_ge(*scaled_before(t, c))
                cols = slice(c * COLS, c * COLS + WIDTH[c] * H)
                acc = t_bank[c % T_BANKS][:, 0:WIDTH[c] * H]
                hi, lo = x1_hi[:, s * P:(s + 1) * P], x1_lo[:, s * P:(s + 1) * P]
                pe.matmul(acc, hi, w1_hi[:, cols], start=True, stop=False)
                pe.matmul(acc, hi, w1_lo[:, cols], start=False, stop=False)
                pe.matmul(acc, lo, w1_hi[:, cols], start=False, stop=True).then_inc(t_mm, 1)

            def group(g, first=False, last=False):
                for s in range(TILES_PER_GROUP):
                    t = g * TILES_PER_GROUP + s
                    pe.wait_ge(x1_lo_ready, g * len(PIECES) + (1 if s < 3 else 2))
                    for c in range(CHUNKS):
                        p = s * CHUNKS + c
                        t_chunk(t, s, c, first and s == 0, g + 1 if p == X0T_AT and not last else None)
                        if c == G_AT and not (first and s < 2):
                            g_product(t - 2, s)
                        if not last:
                            if p == X0T_AT:
                                transpose_x0(g + 1, False)
                            if p in PAIR_AT:
                                pair_product(g + 1, PAIR_AT.index(p))

            def warm_up(n):
                for _ in range(n):
                    pe.matmul(t_bank[T_BANKS - 1][:, :], w_pair[:, 0:P], w_pair[:, 0:COLS], start=True, stop=True)

            pe.wait_ge(w_pair_ready, 1)
            warm_up(WARM_UP[0])
            pe.wait_ge(small_loaded, 16 * SMALL_LOADS)
            transpose_x0(0, True)
            warm_up(WARM_UP[1])
            for b in range(BLOCKS):
                pair_product(0, b)
                warm_up(WARM_UP[2])
            warm_up(WARM_UP[3])
            pe.wait_ge(w_split_lo, 1)
            group(0, first=True)
            with pe.Fori(1, GROUPS - 1) as g:
                group(g)
            group(GROUPS - 1, last=True)
            g_product(TILES - 2, 0)

            def first_layer(m, rows, weights, features, start=False, stop=False):
                return pe.matmul(h1_bank[m][:, :], wt1[0:rows, weights, m * P:(m + 1) * P], features,
                                 start=start, stop=stop)

            pe.wait_ge(wt1_loaded, 16 * WT1_LOADS)
            pe.wait_ge(z0_ready, GROUPS)
            for m in range(M1):
                if m == 2:
                    pe.wait_ge(act_scaled, TILES * NA)
                    pe.wait_ge(dve_scaled, TILES * ND)
                if m == M1 - 1:
                    g_product(TILES - 1, 1)
                first_layer(m, P, 0, z0[:, :], start=True)
                first_layer(m, D, 3, dense[:, :])

            for j in range(F):
                i, k = j // W2_SLOT % SPLIT_W2_SLOTS, j % W2_SLOT
                if k == 0:
                    pe.wait_ge(w2_lo_ready, j // W2_SLOT + 1)
                pe.wait_ge(g_hi_ready, j + 1)
                hi, lo = w2_hi[:, i, k * H:(k + 1) * H], w2_lo[:, i, k * H:(k + 1) * H]
                acc, slot = t_bank[0][:, :], j % SPLIT_G_SLOTS
                pe.matmul(acc, hi, g_hi[:, slot, :], start=j == 0, stop=False)
                pe.matmul(acc, lo, g_hi[:, slot, :], start=False, stop=False)
                pe.wait_ge(g_lo_ready, j + 1)
                pe.matmul(acc, hi, g_lo[:, slot, :], start=False, stop=j == F - 1).then_inc(z2_mm, 1)

            for m in range(M1):
                first_layer(m, P, 1, G[:, F, :])
            pe.wait_ge(z2_ready, 1)
            for m in range(M1):
                first_layer(m, P, 2, z2, stop=True).then_inc(top_mm, 1)
            pe.wait_ge(wt2_loaded, 16)
            for m in range(M2):
                for c in range(M1):
                    pe.wait_ge(h_ready, c + 1)
                    mm = pe.matmul(h2_bank[m][:, :], wt2[:, c, m * P:(m + 1) * P], h1[:, c, :],
                                   start=c == 0, stop=c == M1 - 1)
                mm.then_inc(top_mm, 1)
            for m in range(M2):
                pe.wait_ge(h_ready, M1 + m + 1)
                mm = pe.matmul(small_bank[0:1, :], w3[:, m:m + 1], h2[:, m, :], start=m == 0, stop=m == M2 - 1)
            mm.then_inc(top_mm, 1)

        @block.scalar
        def _(act):
            def copy_x0t(g, s, first):
                t = g * TILES_PER_GROUP + s
                act.wait_ge(x0t_mm, g + 1)
                if not first:
                    prev = t - TILES_PER_GROUP
                    act.wait_ge(act_scaled, (prev + 1) * NA)
                    act.wait_ge(dve_scaled, (prev + 1) * ND)
                    act.wait_ge(diag_ready, prev + 1)
                act.activation(x0t[:, s, 0:F], x0t_psum[:, s, :], ACT.Copy).then_inc(x0t_ready, 1)

            def bias_x1(g, first):
                act.wait_ge(pair_mm, (g + 1) * BLOCKS)
                if not first:
                    act.wait_ge(x1_lo_ready, g * len(PIECES))
                    act.wait_ge(z0_ready, g)
                act.activation(x1[:, :], x1_bank[:, :], ACT.Identity, bias=bias[:, 0:1]).then_inc(x1_ready, 1)

            def split_x1_hi(g, i, first):
                a, b = PIECES[i]
                act.wait_ge(x1_ready, g + 1)
                if not first:
                    act.wait_ge(t_mm, (g - 1) * (TILES_PER_GROUP * CHUNKS) + b * CHUNKS)
                act.activation(x1_hi[:, a * P:b * P], x1[:, a * P:b * P], ACT.Copy).then_inc(x1_hi_ready, 1)

            def copy_g(t, g, s):
                act.wait_ge(g_mm, t + 1)
                act.activation(G[:, :, bass.ds(g * GB + s * TB, TB)].rearrange("p j b -> p b j"),
                               g_psum, ACT.Copy).then_inc(g_copied, 1)

            def scale_chunk(t, s, c, first):
                act.wait_ge(t_mm, t * CHUNKS + (c + 1))
                if c == ACT_CHUNKS[0]:
                    act.wait_ge(x0t_ready, t + 1)
                    if not (first and s < 2):
                        act.wait_ge(summed, (t - 1) * RED)
                for u in range(WIDTH[c]):
                    j = c * UNITS + u
                    last = act.activation(prod[:, s % 2, j, :], t_bank[c % T_BANKS][:, u * H:(u + 1) * H],
                                          ACT.Copy, scale=x0t[:, s, j:j + 1])
                last.then_inc(act_scaled, 1)

            def group(g, first=False, last=False):
                for s in range(TILES_PER_GROUP):
                    t = g * TILES_PER_GROUP + s
                    for c in ACT_CHUNKS:
                        scale_chunk(t, s, c, first)
                        if s == 0 and c == ACT_CHUNKS[1]:
                            split_x1_hi(g, 1, first)
                        if c == 0:
                            if s > 0 and not last:
                                copy_x0t(g + 1, s - 1, False)
                            if s == 0 and not first:
                                copy_x0t(g, TILES_PER_GROUP - 1, False)
                        if c == G_COPY_AT and not (first and s < 2):
                            copy_g(t - 2, g if s >= 2 else g - 1, (s - 2) % TILES_PER_GROUP)
                        if not last:
                            if s == 3 and c == BIAS_AT:
                                bias_x1(g + 1, False)
                                split_x1_hi(g + 1, 0, False)

            act.wait_ge(w_loaded, 16 * 3)
            act.activation(w1_hi[:, :], w1_raw, ACT.Copy).then_inc(w_split_hi, 1)
            act.wait_ge(ones_set, 1)
            act.wait_ge(small_loaded, 16 * SMALL_LOADS)
            for s in range(TILES_PER_GROUP):
                copy_x0t(0, s, True)
            bias_x1(0, True)
            split_x1_hi(0, 0, True)
            group(0, first=True)
            with act.Fori(1, GROUPS - 1) as g:
                group(g)
            group(GROUPS - 1, last=True)
            copy_g(TILES - 2, GROUPS - 1, 2)
            act.wait_ge(t_mm, TILES * CHUNKS)
            for i in range(W2_SLOTS):
                act.wait_ge(w2_loaded[i], 16)
                act.activation(w2_hi[:, i, :], w2_ring[:, i, :], ACT.Copy).then_inc(w2_hi_ready, 1)
            copy_g(TILES - 1, GROUPS - 1, 3)
            act.wait_ge(g_copied, TILES)
            for j in range(F):
                if j >= SPLIT_G_SLOTS:
                    act.wait_ge(z2_mm, j - SPLIT_G_SLOTS + 1)
                act.activation(g_hi[:, j % SPLIT_G_SLOTS, :], G[:, j, :], ACT.Copy).then_inc(g_hi_ready, 1)
            act.wait_ge(bias16_ready, 1)
            act.wait_ge(z2_mm, F)
            act.activation(z2, t_bank[0][:, :], ACT.Identity, bias=bias16[:, 0:1]).then_inc(z2_ready, 1)
            for m in range(M1):
                act.wait_ge(top_mm, m + 1)
                act.activation(h1[:, m, :], h1_bank[m][:, :], ACT.Relu, bias=bias[:, 2 + m:3 + m]).then_inc(h_ready, 1)
            for m in range(M2):
                act.wait_ge(top_mm, M1 + m + 1)
                act.activation(h2[:, m, :], h2_bank[m][:, :], ACT.Relu,
                               bias=bias[:, 2 + M1 + m:3 + M1 + m]).then_inc(h_ready, 1)
            act.wait_ge(top_mm, M1 + M2 + 1)
            act.activation(y, small_bank[0:1, :], ACT.Copy).then_inc(y_ready, 1)

        @block.vector
        def _(dve):
            def form_pairs(g, b, at_start):
                if b == 0:
                    dve.wait_ge(first_ready, (g + 1) * (16 * COPIES))
                else:
                    k = (b - 1) % SECOND_SLOTS
                    dve.wait_ge(second_ready[k], g * (16 * SLOT_USES) + 16 * ((b - 1) // SECOND_SLOTS + 1))
                if not (at_start and b < 2):
                    dve.wait_ge(pair_mm, g * BLOCKS + max(b - 1, 0))
                dve.tensor_tensor(pairs[:, b % 2, :], first[:, :], rep[0:PAIRS, :] if b == 0 else second[:, k, :],
                                  ALU.mult).then_inc(pair_ready, 1)

            def split_x1_lo(g, i):
                a, b = PIECES[i]
                dve.wait_ge(x1_hi_ready, g * len(PIECES) + (i + 1))
                dve.tensor_tensor(x1_lo[:, a * P:b * P], x1[:, a * P:b * P], x1_hi[:, a * P:b * P],
                                  ALU.subtract).then_inc(x1_lo_ready, 1)

            def scale_chunk(t, s, c, first):
                dve.wait_ge(t_mm, t * CHUNKS + (c + 1))
                if c == DVE_CHUNKS[0]:
                    dve.wait_ge(x0t_ready, t + 1)
                    if not (first and s < 2):
                        dve.wait_ge(summed, (t - 1) * RED)
                j, n = c * UNITS, WIDTH[c]
                dve.tensor_tensor(prod[:, s % 2, j:j + n, :],
                                  t_bank[c % T_BANKS][:, 0:n * H].rearrange("p (j h) -> p j h", h=H),
                                  x0t[:, s, j:j + n].unsqueeze(2).to_broadcast([P, n, H]),
                                  ALU.mult).then_inc(dve_scaled, 1)

            def sum_over_j(t, slot, i, first):
                if i == 0:
                    dve.wait_ge(act_scaled, (t + 1) * NA)
                    dve.wait_ge(dve_scaled, (t + 1) * ND)
                    dve.wait_ge(folded, t + 1)
                    if not first:
                        dve.wait_ge(g_mm, t - 1)
                h = slice(i * HR, (i + 1) * HR)
                dve.tensor_reduce(x2[:, slot % 2, h], prod[:, slot % 2, FOLD:, h].rearrange("p j h -> p h j"),
                                  AX.X, ALU.add).then_inc(summed, 1)

            def group(g, first=False, last=False):
                for s in range(TILES_PER_GROUP):
                    t = g * TILES_PER_GROUP + s
                    for c in range(CHUNKS):
                        p = s * CHUNKS + c
                        if c in DVE_CHUNKS:
                            scale_chunk(t, s, c, first)
                        if not last:
                            if p in FORM_AT:
                                form_pairs(g + 1, FORM_AT.index(p), False)
                            if p == X1_LO_AT:
                                split_x1_lo(g + 1, 0)
                        if p == X1_LO_LAST_AT:
                            split_x1_lo(g, 1)
                        if c in SUM_AT and not (first and s == 0):
                            sum_over_j(t - 1, s + 1, SUM_AT.index(c), first and s < 3)

            dve.wait_ge(w_loaded, 16 * 3)
            dve.tensor_tensor(w_pair[:, :], pair_a_raw, pair_b_raw, ALU.add).then_inc(w_pair_ready, 1)
            dve.wait_ge(w_split_hi, 1)
            dve.tensor_tensor(w1_lo[:, :], w1_raw, w1_hi[:, :], ALU.subtract).then_inc(w_split_lo, 1)
            dve.wait_ge(small_loaded, 16 * SMALL_LOADS)
            dve.tensor_scalar(bias16[:, :], bias[:, 1:2], float(D), None, ALU.mult).then_inc(bias16_ready, 1)
            for b in range(BLOCKS):
                form_pairs(0, b, True)
            split_x1_lo(0, 0)
            group(0, first=True)
            with dve.Fori(1, GROUPS - 1) as g:
                group(g)
            group(GROUPS - 1, last=True)
            for i in range(RED):
                sum_over_j(TILES - 1, 1, i, False)
            for j in range(F):
                dve.wait_ge(g_hi_ready, j + 1)
                dve.tensor_tensor(g_lo[:, j % SPLIT_G_SLOTS, :], G[:, j, :], g_hi[:, j % SPLIT_G_SLOTS, :],
                                  ALU.subtract).then_inc(g_lo_ready, 1)


def kernel(**inputs):
    import numpy as np
    import concourse.bacc as _bacc
    from concourse.bass_utils import run_bass_kernel_spmd as _run

    w0 = np.asarray(inputs["L0_rec_W0"]).reshape(H, F, F)

    def in_blocks(w, keep):
        wide = np.concatenate([w, w], axis=0)
        wide = np.ascontiguousarray(np.concatenate([wide, wide], axis=1))
        out = np.zeros((BLOCKS, COPIES, F, H), w.dtype)
        for b in range(BLOCKS):
            for i in range(COPIES):
                if keep(b + i * BLOCKS):
                    out[b, i] = wide[-i * BLOCKS % F:, b:].diagonal()[:, 0:F].T
        return out.reshape(BLOCKS, PAIRS, H).transpose(1, 0, 2).reshape(PAIRS, BLOCKS * H)

    def by_k(w):
        return np.ascontiguousarray(np.asarray(w).reshape(H, F, H).transpose(2, 1, 0)).reshape(H, F * H)

    sample_mask = np.repeat(np.eye(TB, dtype=np.float32), D, axis=0)

    tables = [np.asarray(inputs[f"tbl_{f}"]) for f in range(F)]
    start = np.cumsum([0] + [t.shape[0] for t in tables[:-1]])
    starts = np.zeros(SLOT_ROWS, np.int32)
    starts[:GROUP_ROWS] = np.tile(start, GB)
    ids = np.asarray(inputs["ids"]).reshape(GROUPS, GROUP_ROWS)
    padding = np.zeros((GROUPS, SLOT_ROWS - GROUP_ROWS), ids.dtype)
    ids = np.concatenate([ids, padding], axis=1).reshape(GROUPS, ROW_PARTS, GATHERS).transpose(1, 0, 2)

    arrays = {
        "ids": np.ascontiguousarray(ids).reshape(ROW_PARTS, GROUPS * GATHERS),
        "starts": starts.reshape(ROW_PARTS, GATHERS),
        "table": np.concatenate(tables),
        "dense_t": np.ascontiguousarray(np.asarray(inputs["dense_ctx"]).T),
        "pair_a": in_blocks(w0.transpose(1, 2, 0), lambda shift: 2 * shift < F),
        "pair_b": in_blocks(w0.transpose(2, 1, 0), lambda shift: 0 < 2 * shift < F),
        "w1": by_k(inputs["L0_rec_W1"]),
        "w2": by_k(inputs["L0_rec_W2"]),
        "b0": np.asarray(inputs["L0_rec_b0"]).reshape(H, 1),
        "b1": np.asarray(inputs["L0_rec_b1"]).reshape(1, H),
        "b2": np.asarray(inputs["L0_rec_b2"]).reshape(H, 1),
        "top1": np.ascontiguousarray(inputs["W_top1"]),
        "top_b1": np.ascontiguousarray(np.asarray(inputs["b_top1"]).reshape(M1, P).T),
        "top2": np.ascontiguousarray(inputs["W_top2"]),
        "top_b2": np.ascontiguousarray(np.asarray(inputs["b_top2"]).reshape(M2, P).T),
        "top3": np.ascontiguousarray(np.asarray(inputs["W_top3"]).reshape(M2, P).T),
        "identity": np.eye(F, dtype=np.float32),
        "sample_mask": sample_mask,
    }
    nc = _bacc.Bacc("TRN2", target_bir_lowering=False, num_devices=1)
    aps = {n: nc.dram_tensor(f"in_{n}", a.shape, mybir.dt.from_np(a.dtype), kind="ExternalInput").ap()
           for n, a in arrays.items()}
    out = nc.dram_tensor("out_y", (B, 1), mybir.dt.float32, kind="ExternalOutput").ap()
    tower_program(nc, out=out, **aps)
    r = _run(nc, [{f"in_{n}": a for n, a in arrays.items()}], core_ids=[0])
    return r.results[0]["out_y"]
```
